# Optimizing a Trainium2 kernel written in Bass

```python
import numpy as np
import jax
import jax.numpy as jnp

def _softmax(x, axis=-1):
    return jax.nn.softmax(x, axis=axis)

def _gelu(x):
    return jax.nn.gelu(x, approximate=True)

def _silu(x):
    return jax.nn.silu(x)

def _sigmoid(x):
    return jax.nn.sigmoid(x)

def _layernorm(x, axis=-1, eps=1e-05):
    m = jnp.mean(x, axis=axis, keepdims=True)
    v = jnp.var(x, axis=axis, keepdims=True)
    return (x - m) / jnp.sqrt(v + eps)

def _scatter_add(tgt, idx, src, axis=0):
    return tgt.at[idx].add(src)

def _segment_sum(src, seg, n):
    return jax.ops.segment_sum(src, seg, n)
kernel_name = 'mk_seq_preln_d1_jaxref_r2_288565'

def setup_inputs(seed: int=0):
    np.random.seed(seed)
    _w = jnp.asarray

    def _L0_attn_setup():
        import jax, jax.numpy as jnp
        import numpy as np
        D_MODEL = 512
        N_HEADS = 16
        D_HEAD = D_MODEL // N_HEADS
        EPS = 1e-05

        def _forward(x, ln_g, ln_b, W_qkv, b_qkv, W_gate, b_gate, W_proj, b_proj):
            B, T, D = x.shape
            H, d = (N_HEADS, D_HEAD)
            mu = jnp.mean(x, axis=-1, keepdims=True)
            var = jnp.mean((x - mu) ** 2, axis=-1, keepdims=True)
            x_norm = (x - mu) * jax.lax.rsqrt(var + EPS) * ln_g + ln_b
            qkv = x_norm @ W_qkv + b_qkv
            q, k, v = jnp.split(qkv, 3, axis=-1)
            gate = jax.nn.sigmoid(x @ W_gate + b_gate)
            gate = gate / (jnp.mean(gate, axis=-1, keepdims=True) + EPS)
            q = (q * gate).reshape(B, T, H, d)
            k = (k * gate).reshape(B, T, H, d)
            v = v.reshape(B, T, H, d)
            q = jax.nn.relu(q.astype(jnp.float32)) ** 2 + EPS
            k = jax.nn.relu(k.astype(jnp.float32)) ** 2 + EPS
            v = v.astype(jnp.float32)
            qT = jnp.transpose(q, (1, 0, 2, 3))
            kT = jnp.transpose(k, (1, 0, 2, 3))
            vT = jnp.transpose(v, (1, 0, 2, 3))

            def step(carry, inp):
                kv_s, k_s = carry
                q_t, k_t, v_t = inp
                kv_s = kv_s + k_t[..., :, None] * v_t[..., None, :]
                k_s = k_s + k_t
                num = jnp.einsum('bhd,bhdm->bhm', q_t, kv_s)
                den = jnp.einsum('bhd,bhd->bh', q_t, k_s)[..., None] + EPS
                return ((kv_s, k_s), num / den)
            init = (jnp.zeros((B, H, d, d), jnp.float32), jnp.zeros((B, H, d), jnp.float32))
            _, outT = jax.lax.scan(step, init, (qT, kT, vT))
            out = jnp.transpose(outT, (1, 0, 2, 3)).astype(x.dtype).reshape(B, T, D)
            return out @ W_proj + b_proj
        key = jax.random.key(seed)
        ks = jax.random.split(key, 7)
        B, T = (4, 1024)
        s = 1.0 / np.sqrt(D_MODEL)
        return {'x': jax.random.normal(ks[0], (B, T, D_MODEL), dtype=jnp.float32), 'ln_g': jnp.ones((D_MODEL,), jnp.float32), 'ln_b': jnp.zeros((D_MODEL,), jnp.float32), 'W_qkv': jax.random.normal(ks[1], (D_MODEL, 3 * D_MODEL), jnp.float32) * s, 'b_qkv': jnp.zeros((3 * D_MODEL,), jnp.float32), 'W_gate': jax.random.normal(ks[2], (D_MODEL, D_MODEL), jnp.float32) * s, 'b_gate': jnp.zeros((D_MODEL,), jnp.float32), 'W_proj': jax.random.normal(ks[3], (D_MODEL, D_MODEL), jnp.float32) * s, 'b_proj': jnp.zeros((D_MODEL,), jnp.float32)}
    _L0_attn_in = _L0_attn_setup()

    def _L0_ffn_setup():
        import jax, jax.numpy as jnp
        import numpy as np
        D_MODEL, D_FF, RANK = (512, 2048, 128)
        B, S = (4, 2048)
        key = jax.random.key(seed)
        ks = jax.random.split(key, 7)
        return {'x': jax.random.normal(ks[0], (B, S, D_MODEL), dtype=jnp.float32), 'U1': jax.random.normal(ks[1], (D_MODEL, RANK), dtype=jnp.float32) * 0.02, 'V1': jax.random.normal(ks[2], (RANK, D_FF), dtype=jnp.float32) * 0.02, 'b1': jnp.zeros((D_FF,), dtype=jnp.float32), 'U2': jax.random.normal(ks[3], (D_FF, RANK), dtype=jnp.float32) * 0.02, 'V2': jax.random.normal(ks[4], (RANK, D_MODEL), dtype=jnp.float32) * 0.02, 'b2': jnp.zeros((D_MODEL,), dtype=jnp.float32)}
    _L0_ffn_in = _L0_ffn_setup()
    _d = {'L0_attn_x': _L0_attn_in['x'], 'L0_attn_ln_g': _L0_attn_in['ln_g'], 'L0_attn_ln_b': _L0_attn_in['ln_b'], 'L0_attn_W_qkv': _L0_attn_in['W_qkv'], 'L0_attn_b_qkv': _L0_attn_in['b_qkv'], 'L0_attn_W_gate': _L0_attn_in['W_gate'], 'L0_attn_b_gate': _L0_attn_in['b_gate'], 'L0_attn_W_proj': _L0_attn_in['W_proj'], 'L0_attn_b_proj': _L0_attn_in['b_proj'], 'L0_ffn_U1': _L0_ffn_in['U1'], 'L0_ffn_V1': _L0_ffn_in['V1'], 'L0_ffn_b1': _L0_ffn_in['b1'], 'L0_ffn_U2': _L0_ffn_in['U2'], 'L0_ffn_V2': _L0_ffn_in['V2'], 'L0_ffn_b2': _L0_ffn_in['b2']}
    _x0 = _d['L0_attn_x']
    _d['L0_attn_x'] = jax.random.normal(jax.random.fold_in(jax.random.key(seed), 1), (4, 2048, 512), dtype=_x0.dtype)
    del _x0
    return _d

def reference(L0_attn_x, L0_attn_ln_g, L0_attn_ln_b, L0_attn_W_qkv, L0_attn_b_qkv, L0_attn_W_gate, L0_attn_b_gate, L0_attn_W_proj, L0_attn_b_proj, L0_ffn_U1, L0_ffn_V1, L0_ffn_b1, L0_ffn_U2, L0_ffn_V2, L0_ffn_b2):

    def _L0_attn_ref(x, ln_g, ln_b, W_qkv, b_qkv, W_gate, b_gate, W_proj, b_proj):
        import jax, jax.numpy as jnp
        import numpy as np
        D_MODEL = 512
        N_HEADS = 16
        D_HEAD = D_MODEL // N_HEADS
        EPS = 1e-05

        def _forward(x, ln_g, ln_b, W_qkv, b_qkv, W_gate, b_gate, W_proj, b_proj):
            B, T, D = x.shape
            H, d = (N_HEADS, D_HEAD)
            mu = jnp.mean(x, axis=-1, keepdims=True)
            var = jnp.mean((x - mu) ** 2, axis=-1, keepdims=True)
            x_norm = (x - mu) * jax.lax.rsqrt(var + EPS) * ln_g + ln_b
            qkv = x_norm @ W_qkv + b_qkv
            q, k, v = jnp.split(qkv, 3, axis=-1)
            gate = jax.nn.sigmoid(x @ W_gate + b_gate)
            gate = gate / (jnp.mean(gate, axis=-1, keepdims=True) + EPS)
            q = (q * gate).reshape(B, T, H, d)
            k = (k * gate).reshape(B, T, H, d)
            v = v.reshape(B, T, H, d)
            q = jax.nn.relu(q.astype(jnp.float32)) ** 2 + EPS
            k = jax.nn.relu(k.astype(jnp.float32)) ** 2 + EPS
            v = v.astype(jnp.float32)
            qT = jnp.transpose(q, (1, 0, 2, 3))
            kT = jnp.transpose(k, (1, 0, 2, 3))
            vT = jnp.transpose(v, (1, 0, 2, 3))

            def step(carry, inp):
                kv_s, k_s = carry
                q_t, k_t, v_t = inp
                kv_s = kv_s + k_t[..., :, None] * v_t[..., None, :]
                k_s = k_s + k_t
                num = jnp.einsum('bhd,bhdm->bhm', q_t, kv_s)
                den = jnp.einsum('bhd,bhd->bh', q_t, k_s)[..., None] + EPS
                return ((kv_s, k_s), num / den)
            init = (jnp.zeros((B, H, d, d), jnp.float32), jnp.zeros((B, H, d), jnp.float32))
            _, outT = jax.lax.scan(step, init, (qT, kT, vT))
            out = jnp.transpose(outT, (1, 0, 2, 3)).astype(x.dtype).reshape(B, T, D)
            return out @ W_proj + b_proj
        return _forward(x, ln_g, ln_b, W_qkv, b_qkv, W_gate, b_gate, W_proj, b_proj)

    def _L0_ffn_ref(x, U1, V1, b1, U2, V2, b2):
        import jax, jax.numpy as jnp
        import numpy as np
        D_MODEL, D_FF, RANK = (512, 2048, 128)
        B, S = (4, 2048)
        P = jnp.einsum('bsd,dr->bsr', x, U1)
        H = jax.nn.gelu(jnp.einsum('bsr,rf->bsf', P, V1) + b1)
        Q = jnp.einsum('bsf,fr->bsr', H, U2)
        return jnp.einsum('bsr,rd->bsd', Q, V2) + b2
    x = L0_attn_x
    x = x + _L0_attn_ref(_layernorm(x, axis=-1), L0_attn_ln_g, L0_attn_ln_b, L0_attn_W_qkv, L0_attn_b_qkv, L0_attn_W_gate, L0_attn_b_gate, L0_attn_W_proj, L0_attn_b_proj)
    x = x + _L0_ffn_ref(_layernorm(x, axis=-1), L0_ffn_U1, L0_ffn_V1, L0_ffn_b1, L0_ffn_U2, L0_ffn_V2, L0_ffn_b2)
    return x

_drawn_inputs = setup_inputs


def setup_inputs(seed=0):
    import zlib

    import numpy as np

    out = dict(_drawn_inputs(seed))
    spreads = {'L0_attn_ln_g': (1.0, 0.2),
     'L0_attn_ln_b': (0.0, 0.1),
     'L0_attn_b_qkv': (0.0, 0.1),
     'L0_attn_b_gate': (0.0, 0.8),
     'L0_attn_b_proj': (0.0, 0.1),
     'L0_ffn_b1': (0.0, 0.8),
     'L0_ffn_b2': (0.0, 0.594)}
    factors = {'L0_ffn_U1': 5.451, 'L0_ffn_V1': 5.467, 'L0_ffn_U2': 3.935, 'L0_ffn_V2': 4.232}
    for name, (base, spread) in spreads.items():
        noise = np.random.default_rng([zlib.crc32(name.encode()), seed]).standard_normal(out[name].shape)
        drawn = base * np.exp(spread * noise) if base else spread * noise
        out[name] = jnp.asarray(drawn.astype(out[name].dtype))
    for name, factor in factors.items():
        out[name] = (out[name] * factor).astype(out[name].dtype)
    return out
```

```python
import concourse.bass as bass
from concourse import mybir
from contextlib import ExitStack

F32 = mybir.dt.float32
F32R = mybir.dt.float32r
ALU = mybir.AluOpType
ACT = mybir.ActivationFunctionType
AX = mybir.AxisListType

P = 128
BATCHES = 4
SEQ = 2048
DM = 512
HEAD = 32
DFF = 2048
RANK = 128
KT = DM // P
HPG = P // HEAD
FT = DFF // P
PAIRS = FT // 2
CHUNKS = BATCHES * SEQ // P
POSITIONS = SEQ // P
GROUP = 2 * P
GROUPS = CHUNKS // 2
EPS = 1e-5
NH = DM // HEAD


class Chunk:

    def __init__(self, p, off):
        self.p, self.off = p, off
        self.slot = off % 4
        self.half = off % 2
        m = 4 * p + off if isinstance(p, int) else None
        self.exists = m is None or 0 <= m < CHUNKS
        self.first = m is not None and m < BATCHES
        self.row = (p + off // 4) * P

    def done(self, per=1, i=1):
        return self.p * (4 * per) + (per * self.off + i)

    def dmas(self):
        return self.p * 16 + 16 * (self.off // 4 + 1)


class Group:

    def __init__(self, p, off):
        self.p, self.off = p, off
        g = 2 * p + off if isinstance(p, int) else None
        self.exists = g is None or 0 <= g < GROUPS

    def done(self, per=1, i=1):
        return self.p * (2 * per) + (per * self.off + i)

    def chunk(self, a):
        return Chunk(self.p, 2 * self.off + a)


def wait(eng, sem, value):
    if isinstance(value, int) and value <= 0:
        return
    eng.wait_ge(sem, value)


def steps(eng, step):
    for p in (0, 1):
        for b in range(4):
            step(p, b)
    with eng.Fori(2, POSITIONS - 1) as p:
        for b in range(4):
            step(p, b)
    for p in (POSITIONS - 1, POSITIONS):
        for b in range(4):
            step(p, b)


def block_kernel(nc, x, ln_g, ln_b, w_qkv, b_qkv, w_gate, b_gate, w_proj, b_proj,
                 u1, v1, b1, u2, v2, b2, out, carry_dram):
    ctx = ExitStack()
    with ctx:
        def sb(name, shape, dt=F32):
            return ctx.enter_context(nc.sbuf_tensor(name, shape, dt))

        def sem(name):
            return ctx.enter_context(nc.semaphore(name))

        wx_hi, wx_lo = sb("wx_hi", [P, KT, 4, DM], F32R), sb("wx_lo", [P, KT, 4, DM], F32R)
        wp_hi, wp_lo = sb("wp_hi", [P, KT, DM], F32R), sb("wp_lo", [P, KT, DM], F32R)
        u1_hi, u1_lo = sb("u1_hi", [P, KT, RANK], F32R), sb("u1_lo", [P, KT, RANK], F32R)
        v1_hi, v1_lo = sb("v1_hi", [P, FT, P], F32R), sb("v1_lo", [P, FT, P], F32R)
        u2_hi, u2_lo = sb("u2_hi", [P, FT, RANK], F32R), sb("u2_lo", [P, FT, RANK], F32R)
        v2_hi, v2_lo = sb("v2_hi", [P, DM], F32R), sb("v2_lo", [P, DM], F32R)
        GATE, KEY, QUERY, VALUE = range(4)

        bias = sb("bias", [P, 4, DM])
        bias_proj = sb("bias_proj", [P, DM])
        bias_out = sb("bias_out", [P, DM])
        cols = sb("cols", [P, FT + 2 * KT])
        b1_cols, g_cols, lnb_cols = cols[:, 0:FT], cols[:, FT:FT + KT], cols[:, FT + KT:FT + 2 * KT]
        causal_r = sb("causal", [P, P], F32R)
        causal = causal_r[:, :].bitcast(F32)
        ident = sb("ident", [P, P])
        minus_half, eps_col = sb("minus_half", [P, 1]), sb("eps_col", [P, 1])

        xs = sb("xs", [P, 4, DM])
        x1s = sb("x1s", [P, 4, DM])
        zs = sb("zs", [P, DM])
        gate = sb("gate", [P, DM])
        keys = sb("keys", [P, 2, DM])
        values = sb("values", [P, 2, DM])
        queries = sb("queries", [P, DM])
        key_hi, key_lo = sb("key_hi", [P, DM], F32R), sb("key_lo", [P, DM], F32R)
        key_sums = sb("key_sums", [P, DM])
        vector_rows = gate[0:FT + 2 * KT, 0:P]
        stats, moments = sb("stats", [P, 4, 6]), sb("moments", [P, 4, 2])
        small = sb("small", [P, 4, 6])
        stats1, moments1 = sb("stats1", [P, 6]), sb("moments1", [P, 2])
        small1 = sb("small1", [P, 2])
        gate_sum, gate_scale = sb("gate_sum", [P, 1]), sb("gate_scale", [P, 2])
        den = sb("den", [P, 3, NH])

        zt_hi, zt_lo = sb("zt_hi", [P, KT, P], F32R), sb("zt_lo", [P, KT, P], F32R)
        key_t, query_t = sb("key_t", [P, KT, P]), sb("query_t", [P, KT, P])
        query_bd = sb("query_bd", [P, KT, HPG, P])
        state_bd = sb("state_bd", [P, 4, KT, P])
        probs = sb("probs", [P, 2, HPG * P])
        ot_hi, ot_lo = sb("ot_hi", [P, KT, P], F32R), sb("ot_lo", [P, KT, P], F32R)
        x1t_hi, x1t_lo = sb("x1t_hi", [P, KT, GROUP], F32R), sb("x1t_lo", [P, KT, GROUP], F32R)
        pt_hi, pt_lo = sb("pt_hi", [P, GROUP], F32R), sb("pt_lo", [P, GROUP], F32R)
        qt_hi, qt_lo = pt_hi, pt_lo
        h_full = sb("h_full", [P, 2, 2 * GROUP])
        h_hi, h_lo = sb("h_hi", [P, 2, 2 * GROUP], F32R), sb("h_lo", [P, 2, 2 * GROUP], F32R)
        lnb_wide = probs[:, 0, :].rearrange("p (k n) -> p k n", k=KT)

        def bank(name):
            return ctx.enter_context(nc.psum_tensor(name, [P, DM], F32))

        ps_a = bank("ps_a")
        ps_b = bank("ps_b")
        ps_t = bank("ps_t")
        ps_c = bank("ps_c")
        ps_d = bank("ps_d")
        ps_h = [bank("ps_h0"), bank("ps_h1")]
        ps_q = bank("ps_q")

        names = """vectors_turned cols_ready stage_hi stage_lo stage_bias bias_done consts_pool state_zero query_zero
            biases vectors wide bias_ready
            x_stats x_small z_ready xb_ready tz_done zt_hi_ready zt_ready
            gate_done gate_evac gate_sig gate_scale_ready
            key_done key_steps key_ready key_hi_ready key_lo_ready
            query_done query_steps query_ready value_done value_ready
            sums_done den_steps tk_done key_t_ready tq_done query_t_ready query_bd_ready
            scores_done probs_ready state_done state_ready ot_done ot_hi_ready ot_ready
            y_done x1_steps x1_small z1_ready x1b_ready tx_done x1t_hi_ready x1t_ready
            p_done pt_hi_ready pt_ready h_done h_full_ready h_hi_ready h_lo_ready
            qacc_done qt_hi_ready qt_ready result_done result_ready carry_in""".split()
        s = {n: sem(n) for n in names}
        x_in = [sem(f"x_in{i}") for i in range(4)]
        stored = [sem(f"stored{i}") for i in range(4)]
        carry_out = [sem(f"carry_out{i}") for i in range(4)]
        stage_in = [sem(f"stage_in{i}") for i in range(4)]

        wq_v = w_qkv.rearrange("(k p) n -> k p n", p=P)
        wg_v = w_gate.rearrange("(k p) n -> k p n", p=P)
        tiles = [(wg_v[k, :, :], wx_hi[:, k, GATE, :], wx_lo[:, k, GATE, :], None, None) for k in range(KT)]
        for group, third in ((KEY, 1), (QUERY, 0), (VALUE, 2)):
            tiles += [(wq_v[k, :, third * DM:(third + 1) * DM], wx_hi[:, k, group, :],
                       wx_lo[:, k, group, :], k, group) for k in range(KT)]
        wp_v = w_proj.rearrange("(k p) n -> k p n", p=P)
        tiles += [(wp_v[k, :, :], wp_hi[:, k, :], wp_lo[:, k, :], None, None) for k in range(KT)]
        flat = "p k n -> p (k n)"
        tiles.append((u1.rearrange("(k p) n -> p k n", p=P), u1_hi[:, :, :].rearrange(flat),
                      u1_lo[:, :, :].rearrange(flat), None, None))
        for i in range(FT // 4):
            four = slice(4 * i, 4 * i + 4)
            tiles.append((v1[:, i * DM:(i + 1) * DM], v1_hi[:, four, :].rearrange(flat),
                          v1_lo[:, four, :].rearrange(flat), None, None))
        for i in range(FT // 4):
            four = slice(4 * i, 4 * i + 4)
            tiles.append((u2[i * DM:(i + 1) * DM, :].rearrange("(k p) n -> p k n", p=P),
                          u2_hi[:, four, :].rearrange(flat), u2_lo[:, four, :].rearrange(flat), None, None))
        tiles.append((v2, v2_hi[:, :], v2_lo[:, :], None, None))
        with_bias = [t for t, tile in enumerate(tiles) if tile[4] is not None]
        bias_order = [KEY, QUERY, VALUE]

        block = ctx.enter_context(nc.Block())

        @block.sync
        def _(sp):
            def load_x(c):
                if not c.exists:
                    return
                wait(sp, s["x1_steps"], Chunk(c.p, c.off - 4).done(3, 1))
                sp.dma_start(xs[:, c.slot, :], x[c.slot, bass.ds(c.row, P), :]).then_inc(x_in[c.slot], 16)

            def store(c):
                sp.wait_ge(s["result_ready"], c.done())
                sp.dma_start(out[c.slot, bass.ds(c.row, P), :], x1s[:, c.slot, :]).then_inc(stored[c.slot], 16)

            at = 0
            for v, k in ((b1, FT), (ln_g, KT), (ln_b, KT)):
                sp.dma_start(vector_rows[at:at + k, :], v.rearrange("(k p) -> k p", p=P))\
                    .then_inc(s["vectors"], 16)
                at += k
            for t, (src, _, _, _, _) in enumerate(tiles):
                slot = x1s[:, t % 4, :]
                if t >= 4:
                    sp.wait_ge(s["stage_lo"], t - 3)
                    used = sum(w <= t - 4 for w in with_bias)
                    if used:
                        sp.wait_ge(s["stage_bias"], used)
                dst = slot if len(src.shape) == 2 else slot.rearrange("p (k n) -> p k n", k=src.shape[1])
                sp.dma_start(dst, src).then_inc(stage_in[t % 4], 16)
                if t < 3:
                    load_x(Chunk(0, t))

            def step(p, b):
                if b % 2:
                    g = Group(p, (b - 5) // 2)
                    for a in range(2):
                        if g.exists:
                            store(g.chunk(a))
                c = Chunk(p, b)
                if c.exists:
                    sp.wait_ge(s["den_steps"], c.done(6, 2))
                    sp.dma_start(carry_dram[c.slot:c.slot + 1, :], key_sums[P - 1:P, :])\
                        .then_inc(carry_out[c.slot], 16)
                after = Chunk(p, b + 1)
                if after.exists and not after.first:
                    sp.wait_ge(carry_out[c.slot], c.dmas())
                    sp.dma_start(key_sums[:, :], carry_dram[after.slot:after.slot + 1, :].broadcast_to([P, DM]))\
                        .then_inc(s["carry_in"], 16)
                load_x(Chunk(p, b + 3))

            steps(sp, step)
            for i in range(4):
                sp.wait_ge(stored[i], 16 * POSITIONS)
                sp.wait_ge(carry_out[i], 16 * POSITIONS)

        @block.gpsimd
        def _(pool):
            E = nc.gpsimd
            E.memset(causal, 1.0).then_inc(s["consts_pool"], 1)
            E.memset(ident[:, :], 0.0).then_inc(s["consts_pool"], 1)
            E.memset(minus_half[:, :], -0.5).then_inc(s["consts_pool"], 1)
            E.memset(eps_col[:, :], EPS).then_inc(s["consts_pool"], 1)
            E.memset(probs[:, 0, :], 1.0).then_inc(s["consts_pool"], 1)
            pool.wait_ge(s["consts_pool"], 5)
            E.affine_select(out=causal_r[:, :], in_=causal, compare_op=ALU.is_ge, fill=0.0, base=0,
                            pattern=[[1, P]], channel_multiplier=-1).then_inc(s["consts_pool"], 1)
            E.affine_select(out=ident[:, :], in_=ident[:, :], compare_op=ALU.not_equal, fill=1.0, base=0,
                            pattern=[[-1, P]], channel_multiplier=1).then_inc(s["consts_pool"], 1)
            pool.wait_ge(s["cols_ready"], 1)
            for k in range(KT):
                E.tensor_scalar(lnb_wide[:, k, :], lnb_wide[:, k, :], lnb_cols[:, k:k + 1], 0.0,
                                ALU.mult, ALU.add).then_inc(s["wide"], 1)
            def tiny(out_, a, b, op, sem_):
                E.tensor_tensor(out_, a, b, op).then_inc(sem_, 1)

            def small_stats(c):
                if not c.exists:
                    return
                var, r, done = moments[:, c.slot, 1:2], small[:, c.slot, :], s["x_small"]
                pool.wait_ge(s["x_stats"], c.done(2, 2))
                wait(pool, s["value_ready"], Chunk(c.p, c.off - 4).done())
                tiny(r[:, 0:1], var, eps_col[:, :], ALU.add, done)
                pool.wait_ge(done, c.done(6, 1))
                tiny(r[:, 1:2], r[:, 0:1], minus_half[:, :], ALU.pow, done)
                pool.wait_ge(done, c.done(6, 2))
                tiny(r[:, 2:3], r[:, 1:2], r[:, 1:2], ALU.mult, done)
                pool.wait_ge(done, c.done(6, 3))
                tiny(r[:, 3:4], r[:, 2:3], var, ALU.mult, done)
                pool.wait_ge(done, c.done(6, 4))
                tiny(r[:, 5:6], r[:, 3:4], eps_col[:, :], ALU.add, done)
                pool.wait_ge(done, c.done(6, 5))
                tiny(r[:, 4:5], r[:, 5:6], minus_half[:, :], ALU.pow, done)

            def add_bias(c):
                if c.exists:
                    pool.wait_ge(s["z_ready"], c.done())
                    E.tensor_tensor(xs[:, c.slot, :], xs[:, c.slot, :], bias_proj[:, :], ALU.add)\
                        .then_inc(s["xb_ready"], 1)

            pool.wait_ge(s["consts_pool"], 7)
            small_stats(Chunk(0, 0))
            pool.wait_ge(s["biases"], 16 * 6)
            small_stats(Chunk(0, 1))
            add_bias(Chunk(0, 0))

            def h_tail(g, i):
                pool.wait_ge(s["h_hi_ready"], g.done(PAIRS, i + 1))
                E.tensor_tensor(h_lo[:, i % 2, :], h_full[:, i % 2, :], h_hi[:, i % 2, :].bitcast(F32),
                                ALU.subtract).then_inc(s["h_lo_ready"], 1)

            def step(p, b):
                n, c, d = Chunk(p, b), Chunk(p, b - 1), Chunk(p, b - 2)
                ffn = Group(p, (b - 3) // 2) if b % 2 else Group(p, (b - 4) // 2)
                pairs = range(4) if b % 2 else range(4, 8)
                if d.exists:
                    pool.wait_ge(s["z1_ready"], d.done())
                    E.tensor_tensor(x1s[:, d.slot, :], x1s[:, d.slot, :], bias_out[:, :], ALU.add)\
                        .then_inc(s["x1b_ready"], 1)
                if n.exists:
                    eps_wide = eps_col[:, :].broadcast_to([P, DM])
                    pool.wait_ge(s["key_steps"], n.done(3, 3))
                    E.tensor_tensor(keys[:, n.half, :], keys[:, n.half, :], eps_wide, ALU.add)\
                        .then_inc(s["key_ready"], 1)
                    pool.wait_ge(s["query_steps"], n.done(3, 3))
                    E.tensor_tensor(queries[:, :], queries[:, :], eps_wide, ALU.add)\
                        .then_inc(s["query_ready"], 1)
                add_bias(Chunk(p, b + 1))
                if ffn.exists:
                    h_tail(ffn, pairs[0])
                    h_tail(ffn, pairs[1])
                if n.exists:
                    pool.wait_ge(s["key_hi_ready"], n.done())
                    E.tensor_tensor(key_lo[:, :], keys[:, n.half, :], key_hi[:, :].bitcast(F32),
                                    ALU.subtract).then_inc(s["key_lo_ready"], 1)
                if ffn.exists:
                    h_tail(ffn, pairs[2])
                    h_tail(ffn, pairs[3])
                if c.exists:
                    pool.wait_ge(s["x1_steps"], c.done(3, 3))
                    wait(pool, s["z1_ready"], d.done())
                    tiny(small1[:, 0:1], moments1[:, 1:2], eps_col[:, :], ALU.add, s["x1_small"])
                    pool.wait_ge(s["x1_small"], c.done(2, 1))
                    tiny(small1[:, 1:2], small1[:, 0:1], minus_half[:, :], ALU.pow, s["x1_small"])
                small_stats(Chunk(p, b + 2))

            steps(pool, step)

        @block.scalar
        def _(act):
            E = nc.scalar
            act.dma_start(bias[:, GATE, :], b_gate.rearrange("(a n) -> a n", a=1).broadcast_to([P, DM]))\
                .then_inc(s["biases"], 16)
            b_row = b_qkv.rearrange("(a n) -> a n", a=1)
            for group, third in ((KEY, 1), (QUERY, 0), (VALUE, 2)):
                act.dma_start(bias[:, group, :], b_row[:, third * DM:(third + 1) * DM].broadcast_to([P, DM]))\
                    .then_inc(s["biases"], 16)
            act.dma_start(bias_proj[:, :], b_proj.rearrange("(a n) -> a n", a=1).broadcast_to([P, DM]))\
                .then_inc(s["biases"], 16)
            act.dma_start(bias_out[:, :], b2.rearrange("(a n) -> a n", a=1).broadcast_to([P, DM]))\
                .then_inc(s["biases"], 16)
            act.wait_ge(s["vectors_turned"], 1)
            E.activation(cols[:, :], ps_q[:, 0:FT + 2 * KT], ACT.Copy).then_inc(s["cols_ready"], 1)
            act.wait_ge(s["cols_ready"], 1)
            for t, (_, hi, _, k, _) in enumerate(tiles):
                act.wait_ge(stage_in[t % 4], 16 * (t // 4 + 1))
                scale = 1.0 if k is None else g_cols[:, k:k + 1]
                E.activation(hi, x1s[:, t % 4, :], ACT.Copy, scale=scale).then_inc(s["stage_hi"], 1)

            def z_head(c):
                if c.exists:
                    act.wait_ge(s["tz_done"], c.done())
                    E.activation(zt_hi[:, :, :].rearrange(flat), ps_t[:, :], ACT.Copy)\
                        .then_inc(s["zt_hi_ready"], 1)

            z_head(Chunk(0, 0))

            def gelu(g, i):
                act.wait_ge(s["h_done"], g.done(PAIRS, i + 1))
                if i >= 2:
                    act.wait_ge(s["h_lo_ready"], g.done(PAIRS, i - 1))
                else:
                    wait(act, s["h_lo_ready"], Group(g.p, g.off - 1).done(PAIRS, PAIRS - 1 + i))
                for a in range(2):
                    last = E.activation(h_full[:, i % 2, a * GROUP:(a + 1) * GROUP],
                                        ps_h[i % 2][:, a * GROUP:(a + 1) * GROUP], ACT.Gelu_apprx_tanh,
                                        bias=b1_cols[:, 2 * i + a:2 * i + a + 1])
                last.then_inc(s["h_full_ready"], 1)

            def step(p, b):
                n, c, d = Chunk(p, b), Chunk(p, b - 1), Chunk(p, b - 2)
                ffn = Group(p, (b - 3) // 2) if b % 2 else Group(p, (b - 4) // 2)
                pairs = range(4) if b % 2 else range(4, 8)
                if c.exists:
                    act.wait_ge(s["tq_done"], c.done())
                    E.activation(query_t[:, :, :].rearrange(flat), ps_t[:, :], ACT.Copy)\
                        .then_inc(s["query_t_ready"], 1)
                if n.exists:
                    act.wait_ge(s["gate_evac"], n.done())
                    E.activation(gate[:, :], gate[:, :], ACT.Sigmoid, accum_out=gate_sum[:, :])\
                        .then_inc(s["gate_sig"], 1)
                if c.exists:
                    if c.first:
                        act.wait_ge(s["query_zero"], 1)
                    act.wait_ge(s["query_t_ready"], c.done())
                    for j in range(HPG):
                        rows = slice(HEAD * j, HEAD * (j + 1))
                        last = E.activation(query_bd[rows, :, j, :], query_t[rows, :, :], ACT.Copy)
                    last.then_inc(s["query_bd_ready"], 1)
                if d.exists:
                    act.wait_ge(s["tx_done"], d.done())
                    E.activation(x1t_hi[:, :, d.half * P:(d.half + 1) * P],
                                 ps_t[:, :].rearrange("p (k n) -> p k n", k=KT), ACT.Copy)\
                        .then_inc(s["x1t_hi_ready"], 1)
                if c.exists:
                    act.wait_ge(s["tk_done"], c.done())
                    E.activation(key_t[:, :, :].rearrange(flat), ps_t[:, :], ACT.Copy)\
                        .then_inc(s["key_t_ready"], 1)
                if b % 2 and ffn.exists:
                    act.wait_ge(s["p_done"], ffn.done())
                    E.activation(pt_hi[:, :], ps_c[:, 0:GROUP], ACT.Copy).then_inc(s["pt_hi_ready"], 1)
                if ffn.exists and b % 2 == 0:
                    gelu(ffn, pairs[0])
                if ffn.exists and b % 2:
                    gelu(ffn, pairs[0])
                if ffn.exists:
                    gelu(ffn, pairs[1])
                if n.exists:
                    act.wait_ge(s["key_ready"], n.done())
                    wait(act, s["sums_done"], c.done())
                    E.activation(key_hi[:, :], keys[:, n.half, :], ACT.Copy).then_inc(s["key_hi_ready"], 1)
                if ffn.exists:
                    gelu(ffn, pairs[2])
                if c.exists:
                    act.wait_ge(s["ot_done"], c.done())
                    E.activation(ot_hi[:, :, :].rearrange(flat), ps_b[:, :], ACT.Copy)\
                        .then_inc(s["ot_hi_ready"], 1)
                z_head(Chunk(p, b + 1))
                if ffn.exists:
                    gelu(ffn, pairs[3])
                    if b % 2 == 0:
                        act.wait_ge(s["qacc_done"], ffn.done())
                        E.activation(qt_hi[:, :], ps_q[:, 0:GROUP], ACT.Copy).then_inc(s["qt_hi_ready"], 1)

            steps(act, step)

        @block.vector
        def _(dve):
            E = nc.vector

            def x_stats_wait(c):
                if c.exists:
                    dve.wait_ge(x_in[c.slot], c.dmas())
                    wait(dve, s["x_small"], Chunk(c.p, c.off - 4).done(6, 6))

            def x_stats(c):
                if c.exists:
                    E.bn_stats(stats[:, c.slot, :], xs[:, c.slot, :]).then_inc(s["x_stats"], 1)

            def x_moments(c):
                if c.exists:
                    E.bn_aggr(moments[:, c.slot, :], stats[:, c.slot, :]).then_inc(s["x_stats"], 1)

            def x_norm(c):
                if c.exists:
                    dve.wait_ge(s["x_small"], c.done(6, 2))
                    before = Chunk(c.p, c.off - 3)
                    if before.exists:
                        dve.wait_ge(s["tx_done"], before.done())
                    E.tensor_scalar(zs[:, :], xs[:, c.slot, :], moments[:, c.slot, 0:1], small[:, c.slot, 1:2],
                                    ALU.subtract, ALU.mult).then_inc(s["z_ready"], 1)

            E.memset(query_bd[:, :, :, :].rearrange("p k j n -> p (k j n)"), 0.0).then_inc(s["query_zero"], 1)
            E.memset(state_bd[:, :, :, :].rearrange("p b k n -> p (b k n)"), 0.0).then_inc(s["state_zero"], 1)
            for m in range(2):
                x_stats_wait(Chunk(0, m))
                x_stats(Chunk(0, m))
                dve.wait_ge(s["x_stats"], 2 * m + 1)
                x_moments(Chunk(0, m))
            x_norm(Chunk(0, 0))
            dve.wait_ge(s["cols_ready"], 1)
            for t, (_, hi, lo, k, _) in enumerate(tiles):
                dve.wait_ge(s["stage_hi"], t + 1)
                if k is None:
                    E.tensor_tensor(lo, x1s[:, t % 4, :], hi.bitcast(F32), ALU.subtract)\
                        .then_inc(s["stage_lo"], 1)
                else:
                    E.scalar_tensor_tensor(out=lo, in0=x1s[:, t % 4, :], scalar=g_cols[:, k:k + 1],
                                           in1=hi.bitcast(F32), op0=ALU.mult, op1=ALU.subtract)\
                        .then_inc(s["stage_lo"], 1)
            dve.wait_ge(s["biases"], 16 * 6)
            for i, group in enumerate(bias_order):
                dve.wait_ge(s["bias_done"], i + 1)
                ps = (ps_b, ps_c, ps_d)[i]
                E.tensor_tensor(bias[:, group, :], ps[:, :], bias[:, group, :], ALU.add)\
                    .then_inc(s["bias_ready"], 1)
            dve.wait_ge(s["bias_ready"], 3)

            def z_tail(c):
                if c.exists:
                    dve.wait_ge(s["zt_hi_ready"], c.done())
                    E.tensor_tensor(zt_lo[:, :, :].rearrange(flat), ps_t[:, :],
                                    zt_hi[:, :, :].rearrange(flat).bitcast(F32), ALU.subtract)\
                        .then_inc(s["zt_ready"], 1)

            z_tail(Chunk(0, 0))

            def squared_relu(n, done, chain, ps, group, dst, between=lambda: None):
                dve.wait_ge(done, n.done())
                E.scalar_tensor_tensor(out=dst, in0=ps[:, :], scalar=small[:, n.slot, 4:5],
                                       in1=bias[:, group, :], op0=ALU.mult, op1=ALU.add).then_inc(chain, 1)
                dve.wait_ge(chain, n.done(3, 1))
                E.scalar_tensor_tensor(out=dst, in0=dst, scalar=gate_scale[:, 1:2], in1=gate[:, :],
                                       op0=ALU.mult, op1=ALU.mult).then_inc(chain, 1)
                between()
                dve.wait_ge(chain, n.done(3, 2))
                E.scalar_tensor_tensor(out=dst, in0=dst, scalar=0.0, in1=dst, op0=ALU.max, op1=ALU.mult)\
                    .then_inc(chain, 1)

            def h_head(g, i):
                dve.wait_ge(s["h_full_ready"], g.done(PAIRS, i + 1))
                E.tensor_copy(h_hi[:, i % 2, :], h_full[:, i % 2, :]).then_inc(s["h_hi_ready"], 1)

            def step(p, b):
                n, c, d = Chunk(p, b), Chunk(p, b - 1), Chunk(p, b - 2)
                ffn = Group(p, (b - 3) // 2) if b % 2 else Group(p, (b - 4) // 2)
                pairs = range(4) if b % 2 else range(4, 8)
                def x1t_tail():
                    if d.exists:
                        dve.wait_ge(s["x1t_hi_ready"], d.done())
                        part = slice(d.half * P, (d.half + 1) * P)
                        E.tensor_tensor(x1t_lo[:, :, part], ps_t[:, :].rearrange("p (k n) -> p k n", k=KT),
                                        x1t_hi[:, :, part].bitcast(F32), ALU.subtract).then_inc(s["x1t_ready"], 1)

                if n.exists:
                    dve.wait_ge(s["gate_done"], n.done())
                    E.tensor_tensor(gate[:, :], ps_b[:, :], bias[:, GATE, :], ALU.add)\
                        .then_inc(s["gate_evac"], 1)
                    dve.wait_ge(s["gate_sig"], n.done())
                    E.tensor_scalar(gate_scale[:, 0:1], gate_sum[:, :], 1.0 / DM, EPS, ALU.mult, ALU.add)\
                        .then_inc(s["gate_scale_ready"], 1)
                    dve.wait_ge(s["gate_scale_ready"], n.done(2, 1))
                    E.reciprocal(gate_scale[:, 1:2], gate_scale[:, 0:1]).then_inc(s["gate_scale_ready"], 1)
                    dve.wait_ge(s["gate_scale_ready"], n.done(2, 2))
                    dve.wait_ge(s["x_small"], n.done(6, 6))
                    squared_relu(n, s["key_done"], s["key_steps"], ps_a, KEY, keys[:, n.half, :],
                                 x1t_tail)
                else:
                    x1t_tail()
                if b % 2:
                    g = Group(p, (b - 5) // 2)
                    for a in range(2):
                        if g.exists:
                            r = g.chunk(a)
                            ps = (ps_d, ps_c)[a]
                            dve.wait_ge(s["result_done"], g.done(2, a + 1))
                            dve.wait_ge(s["x1b_ready"], r.done())
                            E.tensor_tensor(x1s[:, r.slot, :], ps[:, :], x1s[:, r.slot, :], ALU.add)\
                                .then_inc(s["result_ready"], 1)
                if n.exists:
                    if c.exists:
                        dve.wait_ge(s["tq_done"], c.done())
                    squared_relu(n, s["query_done"], s["query_steps"], ps_b, QUERY, queries[:, :])
                x_norm(Chunk(p, b + 1))
                if b % 2 and ffn.exists:
                    dve.wait_ge(s["pt_hi_ready"], ffn.done())
                    E.tensor_tensor(pt_lo[:, :], ps_c[:, 0:GROUP], pt_hi[:, :].bitcast(F32), ALU.subtract)\
                        .then_inc(s["pt_ready"], 1)
                if ffn.exists and b % 2 == 0:
                    h_head(ffn, pairs[0])
                if n.exists:
                    dve.wait_ge(s["value_done"], n.done())
                    E.scalar_tensor_tensor(out=values[:, n.half, :], in0=ps_a[:, :],
                                           scalar=small[:, n.slot, 4:5], in1=bias[:, VALUE, :],
                                           op0=ALU.mult, op1=ALU.add).then_inc(s["value_ready"], 1)
                if ffn.exists and b % 2:
                    h_head(ffn, pairs[0])
                if ffn.exists:
                    h_head(ffn, pairs[1])
                if c.exists:
                    for ft in range(KT):
                        ps = (ps_c, ps_d)[ft % 2]
                        dve.wait_ge(s["scores_done"], c.done(KT, ft + 1))
                        E.tensor_tensor(probs[:, ft % 2, :].rearrange("p (j t) -> p j t", j=HPG),
                                        ps[:, :].rearrange("p (j t) -> p j t", j=HPG),
                                        causal.unsqueeze(1).broadcast_to([P, HPG, P]), ALU.mult)\
                            .then_inc(s["probs_ready"], 1)
                        if ft == 1 and ffn.exists:
                            h_head(ffn, pairs[2])
                    dve.wait_ge(s["state_done"], c.done())
                    for j in range(HPG):
                        q = slice(HEAD * j, HEAD * (j + 1))
                        mine = state_bd[q, c.slot, :, q]
                        new = ps_c[:, :].rearrange("p (k n) -> p k n", k=KT)[q, :, q]
                        last = E.tensor_tensor(mine, new, mine, ALU.add)
                    last.then_inc(s["state_ready"], 1)
                    dve.wait_ge(s["ot_hi_ready"], c.done())
                    E.tensor_tensor(ot_lo[:, :, :].rearrange(flat), ps_b[:, :],
                                    ot_hi[:, :, :].rearrange(flat).bitcast(F32), ALU.subtract)\
                        .then_inc(s["ot_ready"], 1)
                elif ffn.exists:
                    h_head(ffn, pairs[2])
                z_tail(Chunk(p, b + 1))
                if ffn.exists:
                    h_head(ffn, pairs[3])
                if n.exists:
                    den_steps = s["den_steps"]
                    dve.wait_ge(s["sums_done"], n.done())
                    if c.exists:
                        dve.wait_ge(carry_out[c.slot], c.dmas())
                    if n.first:
                        E.tensor_copy(key_sums[:, :], ps_b[:, :]).then_inc(den_steps, 1)
                    else:
                        dve.wait_ge(s["carry_in"], Chunk(n.p, n.off - 4).done(16, 16))
                        E.tensor_tensor(key_sums[:, :], ps_b[:, :], key_sums[:, :], ALU.add).then_inc(den_steps, 1)
                    dve.wait_ge(den_steps, n.done(6, 1))
                    dve.wait_ge(s["query_ready"], n.done())
                    E.tensor_tensor(gate[:, :], key_sums[:, :], queries[:, :], ALU.mult).then_inc(den_steps, 1)
                    dve.wait_ge(den_steps, n.done(6, 2))
                    E.tensor_reduce(den[:, 0, :], gate[:, :].rearrange("p (h d) -> p h d", d=HEAD), AX.X,
                                    ALU.add).then_inc(den_steps, 1)
                    dve.wait_ge(den_steps, n.done(6, 3))
                    E.tensor_scalar(den[:, 1, :], den[:, 0, :], EPS, None, ALU.add).then_inc(den_steps, 1)
                    dve.wait_ge(den_steps, n.done(6, 4))
                    E.reciprocal(den[:, 2, :], den[:, 1, :]).then_inc(den_steps, 1)
                    dve.wait_ge(den_steps, n.done(6, 5))
                    by_head = queries[:, :].rearrange("p (h d) -> p h d", d=HEAD)
                    E.tensor_tensor(by_head, by_head, den[:, 2, :].unsqueeze(2).broadcast_to([P, NH, HEAD]),
                                    ALU.mult).then_inc(den_steps, 1)
                if c.exists:
                    dve.wait_ge(s["y_done"], c.done())
                    dve.wait_ge(s["xb_ready"], c.done())
                    before = Chunk(c.p, c.off - 4)
                    if before.exists:
                        dve.wait_ge(stored[c.slot], before.dmas())
                    E.tensor_tensor(x1s[:, c.slot, :], ps_a[:, :], xs[:, c.slot, :], ALU.add)\
                        .then_inc(s["x1_steps"], 1)
                    dve.wait_ge(s["x1_steps"], c.done(3, 1))
                    E.bn_stats(stats1[:, :], x1s[:, c.slot, :]).then_inc(s["x1_steps"], 1)
                    dve.wait_ge(s["x1_steps"], c.done(3, 2))
                    wait(dve, s["x1_small"], d.done(2, 2))
                ahead = Chunk(p, b + 2)
                x_stats_wait(ahead)
                x_stats(ahead)
                if c.exists:
                    E.bn_aggr(moments1[:, :], stats1[:, :]).then_inc(s["x1_steps"], 1)
                if ahead.exists:
                    dve.wait_ge(s["x_stats"], ahead.done(2, 1))
                if c.exists:
                    dve.wait_ge(s["x1_small"], c.done(2, 2))
                    after = Chunk(p, b + 1)
                    if after.exists:
                        dve.wait_ge(s["tz_done"], after.done())
                    elif d.exists:
                        dve.wait_ge(s["tx_done"], d.done())
                    E.tensor_scalar(zs[:, :], x1s[:, c.slot, :], moments1[:, 0:1], small1[:, 1:2],
                                    ALU.subtract, ALU.mult).then_inc(s["z1_ready"], 1)
                x_moments(ahead)
                if ffn.exists and b % 2 == 0:
                    dve.wait_ge(s["qt_hi_ready"], ffn.done())
                    E.tensor_tensor(qt_lo[:, :], ps_q[:, 0:GROUP], qt_hi[:, :].bitcast(F32), ALU.subtract)\
                        .then_inc(s["qt_ready"], 1)

            steps(dve, step)

        @block.tensor
        def _(pe):
            E = nc.tensor

            def product(ps, weights, moving, start=True, stop=True):
                last = len(weights) - 1
                for i, ((wh, wl), (mh, ml)) in enumerate(zip(weights, moving)):
                    E.matmul(ps, wh, mh, start=start and i == 0, stop=False)
                    E.matmul(ps, wh, ml, start=False, stop=False)
                    mm = E.matmul(ps, wl, mh, start=False, stop=stop and i == last)
                return mm

            def transpose4(src, done):
                for k in range(KT):
                    mm = E.transpose(ps_t[:, k * P:(k + 1) * P], src[:, k * P:(k + 1) * P], ident[:, :])
                mm.then_inc(done, 1)

            def project(group, ps, done):
                product(ps[:, :], [(zt_hi[:, k, :], zt_lo[:, k, :]) for k in range(KT)],
                        [(wx_hi[:, k, group, :], wx_lo[:, k, group, :]) for k in range(KT)]).then_inc(done, 1)

            pe.wait_ge(s["vectors"], 48)
            pe.wait_ge(s["consts_pool"], 7)
            rows = FT + 2 * KT
            E.transpose(ps_q[:, 0:rows], vector_rows, ident[0:rows, 0:rows]).then_inc(s["vectors_turned"], 1)
            pe.wait_ge(s["wide"], KT)
            for i, t in enumerate(with_bias):
                k, group = tiles[t][3], tiles[t][4]
                pe.wait_ge(stage_in[t % 4], 16 * (t // 4 + 1))
                ps = (ps_b, ps_c, ps_d)[bias_order.index(group)]
                mm = E.matmul(ps[:, :], lnb_wide[:, k, :], x1s[:, t % 4, :], start=k == 0, stop=k == KT - 1)
                mm.then_inc(s["stage_bias"], 1)
                if k == KT - 1:
                    pe.wait_ge(s["stage_bias"], i + 1)
                    E.transpose(ps_q[:, 0:P], ident[:, :], ident[:, :]).then_inc(s["bias_done"], 1)

            def tz(c):
                if not c.exists:
                    return
                pe.wait_ge(s["z_ready"], c.done())
                before = Chunk(c.p, c.off - 2)
                if before.exists:
                    pe.wait_ge(s["key_t_ready"], before.done())
                transpose4(zs, s["tz_done"])

            tz(Chunk(0, 0))

            def h_pair(g, i):
                if i == 0:
                    pe.wait_ge(s["pt_ready"], g.done())
                if i >= 2:
                    pe.wait_ge(s["h_full_ready"], g.done(PAIRS, i - 1))
                else:
                    wait(pe, s["h_full_ready"], Group(g.p, g.off - 1).done(PAIRS, PAIRS - 1 + i))
                for a in range(2):
                    j = 2 * i + a
                    mm = product(ps_h[i % 2][:, a * GROUP:(a + 1) * GROUP], [(v1_hi[:, j, :], v1_lo[:, j, :])],
                                 [(pt_hi[:, :], pt_lo[:, :])])
                mm.then_inc(s["h_done"], 1)

            def q_pair(g, i):
                pe.wait_ge(s["h_lo_ready"], g.done(PAIRS, i + 1))
                if i == 0:
                    wait(pe, s["qt_ready"], Group(g.p, g.off - 1).done())
                cols = [slice(a * GROUP, (a + 1) * GROUP) for a in range(2)]
                mm = product(ps_q[:, 0:GROUP], [(u2_hi[:, 2 * i + a, :], u2_lo[:, 2 * i + a, :]) for a in range(2)],
                             [(h_hi[:, i % 2, q], h_lo[:, i % 2, q]) for q in cols],
                             start=i == 0, stop=i == PAIRS - 1)
                if i == PAIRS - 1:
                    mm.then_inc(s["qacc_done"], 1)

            def step(p, b):
                n, c, d = Chunk(p, b), Chunk(p, b - 1), Chunk(p, b - 2)
                ffn = Group(p, (b - 3) // 2) if b % 2 else Group(p, (b - 4) // 2)
                result = Group(p, (b - 5) // 2) if b % 2 else None
                pairs = range(4) if b % 2 else range(4, 8)
                if n.exists:
                    pe.wait_ge(s["zt_ready"], n.done())
                    if c.exists:
                        pe.wait_ge(s["den_steps"], c.done(6, 1))
                    else:
                        pe.wait_ge(s["stage_lo"], len(tiles))
                        pe.wait_ge(s["bias_ready"], 3)
                    project(GATE, ps_b, s["gate_done"])
                if c.exists:
                    pe.wait_ge(s["den_steps"], c.done(6, 6))
                    if n.exists:
                        pe.wait_ge(s["zt_ready"], n.done())
                    else:
                        pe.wait_ge(s["key_t_ready"], d.done())
                    transpose4(queries, s["tq_done"])
                if n.exists:
                    if d.exists:
                        pe.wait_ge(s["x1_steps"], d.done(3, 1))
                    project(KEY, ps_a, s["key_done"])
                if d.exists:
                    pe.wait_ge(s["z1_ready"], d.done())
                    if c.exists:
                        pe.wait_ge(s["query_t_ready"], c.done())
                    else:
                        pe.wait_ge(s["key_t_ready"], d.done())
                    transpose4(zs, s["tx_done"])
                if result is not None and result.exists:
                    pe.wait_ge(s["qt_ready"], result.done())
                    for a in range(2):
                        cols = slice(a * P, (a + 1) * P)
                        ps = (ps_d, ps_c)[a]
                        before = d if d.exists else Chunk(0, CHUNKS - 1)
                        if a == 0:
                            pe.wait_ge(s["probs_ready"], before.done(KT, KT))
                        else:
                            pe.wait_ge(s["state_ready"], before.done())
                        product(ps[:, :], [(qt_hi[:, cols], qt_lo[:, cols])], [(v2_hi[:, :], v2_lo[:, :])])\
                            .then_inc(s["result_done"], 1)
                if n.exists:
                    pe.wait_ge(s["gate_evac"], n.done())
                    project(QUERY, ps_b, s["query_done"])
                if c.exists:
                    if d.exists:
                        pe.wait_ge(s["x1t_ready"], d.done())
                    else:
                        pe.wait_ge(s["query_t_ready"], c.done())
                    pe.wait_ge(s["key_ready"], c.done())
                    transpose4(keys[:, c.half, :], s["tk_done"])
                if b % 2 and ffn.exists:
                    pe.wait_ge(s["x1t_ready"], d.done())
                    pe.wait_ge(s["state_ready"], d.done())
                    if result.exists:
                        pe.wait_ge(s["result_ready"], result.chunk(1).done())
                    product(ps_c[:, 0:GROUP], [(u1_hi[:, k, :], u1_lo[:, k, :]) for k in range(KT)],
                            [(x1t_hi[:, k, :], x1t_lo[:, k, :]) for k in range(KT)]).then_inc(s["p_done"], 1)
                if ffn.exists and b % 2 == 0:
                    h_pair(ffn, pairs[0])
                if n.exists:
                    pe.wait_ge(s["key_steps"], n.done(3, 1))
                    project(VALUE, ps_a, s["value_done"])
                if ffn.exists and b % 2:
                    h_pair(ffn, pairs[0])
                if ffn.exists:
                    h_pair(ffn, pairs[1])
                if c.exists:
                    pe.wait_ge(s["query_bd_ready"], c.done())
                    pe.wait_ge(s["key_t_ready"], c.done())
                    if n.exists:
                        pe.wait_ge(s["query_steps"], n.done(3, 1))
                    else:
                        pe.wait_ge(s["den_steps"], c.done(6, 1))
                    if not c.first:
                        pe.wait_ge(s["state_ready"], Chunk(c.p, c.off - 4).done())
                        for ft in range(KT):
                            E.matmul(ps_b[:, ft * P:(ft + 1) * P], state_bd[:, c.slot, ft, :],
                                     query_t[:, ft, :], start=ft == 0, stop=False, skip_group_check=True)

                    def scores(ft):
                        ps = (ps_c, ps_d)[ft % 2]
                        if ft >= 2:
                            pe.wait_ge(s["probs_ready"], c.done(KT, ft - 1))
                        else:
                            if result is not None and result.exists:
                                pe.wait_ge(s["result_ready"], result.chunk(1 - ft).done())
                            if b % 2 and ffn.exists and ft == 0:
                                pe.wait_ge(s["pt_ready"], ffn.done())
                            if d.exists:
                                if ft == 0:
                                    pe.wait_ge(s["state_ready"], d.done())
                                else:
                                    pe.wait_ge(s["probs_ready"], d.done(KT, KT))
                        E.matmul(ps[:, :], key_t[:, ft, :], query_bd[:, ft, :, :].rearrange("p j t -> p (j t)"),
                                 start=True, stop=True).then_inc(s["scores_done"], 1)

                    def mix(ft):
                        pe.wait_ge(s["probs_ready"], c.done(KT, ft + 1))
                        for j in range(HPG):
                            h = ft * HPG + j
                            mm = E.matmul(ps_b[HEAD * j:HEAD * (j + 1), ft * P:(ft + 1) * P],
                                          values[:, c.half, h * HEAD:(h + 1) * HEAD],
                                          probs[:, ft % 2, j * P:(j + 1) * P],
                                          start=c.first and ft == 0, stop=True,
                                          tile_position=(0, HEAD * j), skip_group_check=True)
                        return mm

                    scores(0)
                    scores(1)
                    pe.wait_ge(s["value_ready"], c.done())
                    mix(0)
                if ffn.exists:
                    q_pair(ffn, pairs[0])
                    h_pair(ffn, pairs[2])
                if c.exists:
                    scores(2)
                    mix(1)
                if ffn.exists:
                    q_pair(ffn, pairs[1])
                if c.exists:
                    scores(3)
                    mix(2)
                    pe.wait_ge(s["probs_ready"], c.done(KT, 3))
                    for ft in range(KT):
                        cols = slice(ft * P, (ft + 1) * P)
                        mm = E.matmul(ps_c[:, cols], keys[:, c.half, cols], values[:, c.half, cols],
                                      start=True, stop=True)
                    mm.then_inc(s["state_done"], 1)
                    mix(3).then_inc(s["ot_done"], 1)
                tz(Chunk(p, b + 1))
                if ffn.exists:
                    h_pair(ffn, pairs[3])
                    q_pair(ffn, pairs[2])
                if n.exists:
                    if c.exists:
                        pe.wait_ge(s["ot_ready"], c.done())
                    pe.wait_ge(s["key_lo_ready"], n.done())
                    E.matmul(ps_b[:, :], causal_r[:, :], key_hi[:, :], start=True, stop=False)
                    E.matmul(ps_b[:, :], causal_r[:, :], key_lo[:, :], start=False, stop=True)\
                        .then_inc(s["sums_done"], 1)
                if c.exists:
                    pe.wait_ge(s["ot_ready"], c.done())
                    if n.exists:
                        pe.wait_ge(s["value_ready"], n.done())
                    elif d.exists:
                        pe.wait_ge(s["x1_steps"], d.done(3, 1))
                    product(ps_a[:, :], [(ot_hi[:, k, :], ot_lo[:, k, :]) for k in range(KT)],
                            [(wp_hi[:, k, :], wp_lo[:, k, :]) for k in range(KT)]).then_inc(s["y_done"], 1)
                if ffn.exists:
                    q_pair(ffn, pairs[3])

            steps(pe, step)


_INS = ['L0_attn_x', 'L0_attn_ln_g', 'L0_attn_ln_b', 'L0_attn_W_qkv', 'L0_attn_b_qkv', 'L0_attn_W_gate',
        'L0_attn_b_gate', 'L0_attn_W_proj', 'L0_attn_b_proj', 'L0_ffn_U1', 'L0_ffn_V1', 'L0_ffn_b1',
        'L0_ffn_U2', 'L0_ffn_V2', 'L0_ffn_b2']


def kernel(**inputs):
    import numpy as _np
    import concourse.bacc as _bacc
    from concourse import mybir as _mybir
    from concourse.bass_utils import run_bass_kernel_spmd as _run

    nc = _bacc.Bacc("TRN2", target_bir_lowering=False, num_devices=1, dynamic_dma_scratch_size=64)
    arrays, args = {}, []
    for name in _INS:
        a = _np.ascontiguousarray(inputs[name])
        arrays[name] = a
        args.append(nc.dram_tensor(name, a.shape, _mybir.dt.from_np(a.dtype), kind="ExternalInput").ap())
    out = nc.dram_tensor("out", (BATCHES, SEQ, DM), _mybir.dt.float32, kind="ExternalOutput").ap()
    carry_dram = nc.dram_tensor("carry_rows", (BATCHES, DM), _mybir.dt.float32, kind="Internal").ap()
    block_kernel(nc, *args, out, carry_dram)
    r = _run(nc, [arrays], core_ids=[0])
    return r.results[0]["out"]
```

```python
import concourse.bass as bass
from concourse import mybir
from contextlib import ExitStack

F32 = mybir.dt.float32
F32R = mybir.dt.float32r
ALU = mybir.AluOpType
ACT = mybir.ActivationFunctionType
AX = mybir.AxisListType

P = 128
BATCHES = 4
SEQ = 2048
DM = 512
HEAD = 32
DFF = 2048
RANK = 128
KT = DM // P
HPG = P // HEAD
FT = DFF // P
PAIRS = FT // 2
CHUNKS = BATCHES * SEQ // P
POSITIONS = SEQ // P
GROUP = 2 * P
GROUPS = CHUNKS // 2
EPS = 1e-5
NH = DM // HEAD


class Chunk:

    def __init__(self, p, off):
        self.p, self.off = p, off
        self.slot = off % 4
        self.half = off % 2
        m = 4 * p + off if isinstance(p, int) else None
        self.exists = m is None or 0 <= m < CHUNKS
        self.first = m is not None and m < BATCHES
        self.row = (p + off // 4) * P

    def done(self, per=1, i=1):
        return self.p * (4 * per) + (per * self.off + i)

    def dmas(self):
        return self.p * 16 + 16 * (self.off // 4 + 1)


class Group:

    def __init__(self, p, off):
        self.p, self.off = p, off
        g = 2 * p + off if isinstance(p, int) else None
        self.exists = g is None or 0 <= g < GROUPS

    def done(self, per=1, i=1):
        return self.p * (2 * per) + (per * self.off + i)

    def chunk(self, a):
        return Chunk(self.p, 2 * self.off + a)


def wait(eng, sem, value):
    if isinstance(value, int) and value <= 0:
        return
    eng.wait_ge(sem, value)


def is_last(p):
    return isinstance(p, int) and p == POSITIONS


def steps(eng, step):
    for p in (0, 1):
        for b in range(4):
            step(p, b)
    with eng.Fori(2, POSITIONS - 1) as p:
        for b in range(4):
            step(p, b)
    for p in (POSITIONS - 1, POSITIONS):
        for b in range(4):
            step(p, b)


def block_kernel(nc, x, ln_g, ln_b, w_qkv, b_qkv, w_gate, b_gate, w_proj, b_proj,
                 u1, v1, b1, u2, v2, b2, out, carry_dram):
    ctx = ExitStack()
    with ctx:
        def sb(name, shape, dt=F32):
            return ctx.enter_context(nc.sbuf_tensor(name, shape, dt))

        def sb_over(name, over, shape, dt):
            with nc.sbuf_tensor(name, shape, F32) as first:
                pass
            return first, sb(over, shape, dt)

        def sem(name):
            return ctx.enter_context(nc.semaphore(name))

        wx_hi, wx_lo = sb("wx_hi", [P, KT, 4, DM], F32R), sb("wx_lo", [P, KT, 4, DM], F32R)
        wp_hi, wp_lo = sb("wp_hi", [P, KT, DM], F32R), sb("wp_lo", [P, KT, DM], F32R)
        u1_hi, u1_lo = sb("u1_hi", [P, KT, RANK], F32R), sb("u1_lo", [P, KT, RANK], F32R)
        v1_hi, v1_lo = sb("v1_hi", [P, FT, P], F32R), sb("v1_lo", [P, FT, P], F32R)
        u2_hi, u2_lo = sb("u2_hi", [P, FT, RANK], F32R), sb("u2_lo", [P, FT, RANK], F32R)
        v2_hi, v2_lo = sb("v2_hi", [P, DM], F32R), sb("v2_lo", [P, DM], F32R)
        GATE, KEY, QUERY, VALUE = range(4)

        bias = sb("bias", [P, 4, DM])
        bias_proj = sb("bias_proj", [P, DM])
        bias_out = sb("bias_out", [P, DM])
        cols = sb("cols", [P, FT + 2 * KT])
        b1_cols, g_cols, lnb_cols = cols[:, 0:FT], cols[:, FT:FT + KT], cols[:, FT + KT:FT + 2 * KT]
        causal_r = sb("causal", [P, P], F32R)
        causal = causal_r[:, :].bitcast(F32)
        ident = sb("ident", [P, P])
        minus_half, eps_col = sb("minus_half", [P, 1]), sb("eps_col", [P, 1])

        xs = sb("xs", [P, 4, DM])
        x1s = sb("x1s", [P, 4, DM])
        zs = sb("zs", [P, DM])
        gate = sb("gate", [P, DM])
        keys = sb("keys", [P, 2, DM])
        values = sb("values", [P, 2, DM])
        queries = sb("queries", [P, DM])
        query_t, key_hi = sb_over("query_t", "key_hi", [P, DM], F32R)
        query_t = query_t[:, :].rearrange("p (k n) -> p k n", k=KT)
        key_lo = sb("key_lo", [P, DM], F32R)
        key_sums = sb("key_sums", [P, DM])
        vector_rows = gate[0:FT + 2 * KT, 0:P]
        stats, moments = sb("stats", [P, 4, 6]), sb("moments", [P, 4, 2])
        small = sb("small", [P, 4, 6])
        stats1, moments1 = sb("stats1", [P, 6]), sb("moments1", [P, 2])
        small1 = sb("small1", [P, 2])
        gate_sum, gate_scale = sb("gate_sum", [P, 1]), sb("gate_scale", [P, 2])
        den = sb("den", [P, 3, NH])

        zt_hi, zt_lo = sb("zt_hi", [P, KT, P], F32R), sb("zt_lo", [P, KT, P], F32R)
        key_t_hi, key_t_lo = sb("key_t_hi", [P, KT, P], F32R), sb("key_t_lo", [P, KT, P], F32R)
        ot_hi, ot_lo = key_t_hi, key_t_lo
        query_bd_hi = sb("query_bd_hi", [P, KT, HPG, P], F32R)
        query_bd_lo = sb("query_bd_lo", [P, KT, HPG, P], F32R)
        state_bd = sb("state_bd", [P, 4, KT, P])
        probs = sb("probs", [P, 2, HPG * P])
        x1t_hi, x1t_lo = sb("x1t_hi", [P, KT, GROUP], F32R), sb("x1t_lo", [P, KT, GROUP], F32R)
        pt_hi, pt_lo = sb("pt_hi", [P, GROUP], F32R), sb("pt_lo", [P, GROUP], F32R)
        qt_hi, qt_lo = pt_hi, pt_lo
        h_hi = sb("h_hi", [P, 2, 2 * GROUP], F32R)
        h_full, h_lo = sb_over("h_full", "h_lo", [P, 2, 2 * GROUP], F32R)
        lnb_wide = probs[:, 0, :].rearrange("p (k n) -> p k n", k=KT)

        def bank(name):
            return ctx.enter_context(nc.psum_tensor(name, [P, DM], F32))

        ps_a = bank("ps_a")
        ps_b = bank("ps_b")
        ps_t = bank("ps_t")
        ps_c = bank("ps_c")
        ps_d = bank("ps_d")
        ps_h = [bank("ps_h0"), bank("ps_h1")]
        ps_q = bank("ps_q")

        names = """vectors_turned cols_ready stage_hi stage_lo stage_bias consts_pool state_zero query_zero
            biases late_biases vectors wide bias_ready
            x_stats x_small z_ready xb_ready tz_done zt_hi_ready zt_ready
            gate_done gate_evac gate_sig gate_scale_ready
            key_done key_steps key_ready key_hi_ready key_lo_ready
            query_done query_steps query_ready value_done value_ready
            sums_done den_steps tk_done key_t_hi_ready key_t_ready tq_done query_t_ready
            query_bd_hi_ready query_bd_ready
            scores_done earlier_done probs_ready state_done state_ready ot_done ot_hi_ready ot_ready
            y_done x1_steps x1_small z1_ready x1b_ready tx_done x1t_hi_ready x1t_ready
            p_done pt_hi_ready pt_ready h_done h_full_ready h_hi_ready h_lo_ready
            qacc_done qt_hi_ready qt_ready result_done result_ready carry_in""".split()
        s = {n: sem(n) for n in names}
        x_in = [sem(f"x_in{i}") for i in range(4)]
        stored = [sem(f"stored{i}") for i in range(4)]
        carry_out = [sem(f"carry_out{i}") for i in range(4)]
        stage_in = [sem(f"stage_in{i}") for i in range(6)]

        wq_v = w_qkv.rearrange("(k p) n -> k p n", p=P)
        wg_v = w_gate.rearrange("(k p) n -> k p n", p=P)
        tiles = [(wg_v[k, :, :], wx_hi[:, k, GATE, :], wx_lo[:, k, GATE, :], None, None) for k in range(KT)]
        for group, third in ((KEY, 1), (QUERY, 0), (VALUE, 2)):
            tiles += [(wq_v[k, :, third * DM:(third + 1) * DM], wx_hi[:, k, group, :],
                       wx_lo[:, k, group, :], k, group) for k in range(KT)]
        wp_v = w_proj.rearrange("(k p) n -> k p n", p=P)
        tiles += [(wp_v[k, :, :], wp_hi[:, k, :], wp_lo[:, k, :], None, None) for k in range(KT)]
        flat = "p k n -> p (k n)"
        tiles.append((u1.rearrange("(k p) n -> p k n", p=P), u1_hi[:, :, :].rearrange(flat),
                      u1_lo[:, :, :].rearrange(flat), None, None))
        for i in range(FT // 4):
            four = slice(4 * i, 4 * i + 4)
            tiles.append((v1[:, i * DM:(i + 1) * DM], v1_hi[:, four, :].rearrange(flat),
                          v1_lo[:, four, :].rearrange(flat), None, None))
        for i in range(FT // 4):
            four = slice(4 * i, 4 * i + 4)
            tiles.append((u2[i * DM:(i + 1) * DM, :].rearrange("(k p) n -> p k n", p=P),
                          u2_hi[:, four, :].rearrange(flat), u2_lo[:, four, :].rearrange(flat), None, None))
        tiles.append((v2, v2_hi[:, :], v2_lo[:, :], None, None))
        FIRST = 4 * KT
        early_tiles = range(FIRST, FIRST + 3)
        late_tiles = [range(FIRST + 3, FIRST + 9), range(FIRST + 9, FIRST + 12), range(FIRST + 12, len(tiles))]

        def stage(t):
            i = t % 6
            return x1s[:, i, :] if i < 4 else h_full[:, i - 4, :]

        with_bias = [t for t, tile in enumerate(tiles) if tile[4] is not None]
        bias_order = [KEY, QUERY, VALUE]
        bias_banks = [ps_c, ps_d, ps_h[0]]

        block = ctx.enter_context(nc.Block())

        @block.sync
        def _(sp):
            def load_x(c):
                if not c.exists:
                    return
                wait(sp, s["x1_steps"], Chunk(c.p, c.off - 4).done(3, 1))
                sp.dma_start(xs[:, c.slot, :], x[c.slot, bass.ds(c.row, P), :]).then_inc(x_in[c.slot], 16)

            def store(c):
                sp.wait_ge(s["result_ready"], c.done())
                sp.dma_start(out[c.slot, bass.ds(c.row, P), :], x1s[:, c.slot, :]).then_inc(stored[c.slot], 16)

            at = 0
            for v, k in ((b1, FT), (ln_g, KT), (ln_b, KT)):
                sp.dma_start(vector_rows[at:at + k, :], v.rearrange("(k p) -> k p", p=P))\
                    .then_inc(s["vectors"], 16)
                at += k
            def load_tiles(ts):
                for t in ts:
                    src, slot = tiles[t][0], stage(t)
                    if t >= 6:
                        sp.wait_ge(s["stage_lo"], t - 5)
                        used = sum(w <= t - 6 for w in with_bias)
                        if used:
                            sp.wait_ge(s["stage_bias"], used)
                    dst = slot if len(src.shape) == 2 else slot.rearrange("p (k n) -> p k n", k=src.shape[1])
                    sp.dma_start(dst, src).then_inc(stage_in[t % 6], 16)

            load_x(Chunk(0, 0))
            load_tiles(range(8))
            load_x(Chunk(0, 1))
            load_tiles(range(8, FIRST))
            load_x(Chunk(0, 2))
            load_tiles(range(FIRST, FIRST + 6))

            def step(p, b):
                if isinstance(p, int) and 4 * p + b < 2:
                    load_tiles((range(FIRST + 6, FIRST + 9), range(FIRST + 9, len(tiles)))[b])
                if b % 2:
                    g = Group(p, (b - 5) // 2)
                    for a in range(2):
                        if g.exists:
                            store(g.chunk(a))
                c = Chunk(p, b)
                if c.exists:
                    sp.wait_ge(s["den_steps"], c.done(6, 2))
                    sp.dma_start(carry_dram[c.slot:c.slot + 1, :], key_sums[P - 1:P, :])\
                        .then_inc(carry_out[c.slot], 16)
                after = Chunk(p, b + 1)
                if after.exists and not after.first:
                    sp.wait_ge(carry_out[c.slot], c.dmas())
                    sp.dma_start(key_sums[:, :], carry_dram[after.slot:after.slot + 1, :].broadcast_to([P, DM]))\
                        .then_inc(s["carry_in"], 16)
                load_x(Chunk(p, b + 3))

            steps(sp, step)
            for i in range(4):
                sp.wait_ge(stored[i], 16 * POSITIONS)
                sp.wait_ge(carry_out[i], 16 * POSITIONS)

        @block.gpsimd
        def _(pool):
            E = nc.gpsimd
            E.memset(causal, 1.0).then_inc(s["consts_pool"], 1)
            E.memset(ident[:, :], 0.0).then_inc(s["consts_pool"], 1)
            E.memset(minus_half[:, :], -0.5).then_inc(s["consts_pool"], 1)
            E.memset(eps_col[:, :], EPS).then_inc(s["consts_pool"], 1)
            E.memset(probs[:, 0, :], 1.0).then_inc(s["consts_pool"], 1)
            pool.wait_ge(s["consts_pool"], 5)
            E.affine_select(out=causal_r[:, :], in_=causal, compare_op=ALU.is_ge, fill=0.0, base=0,
                            pattern=[[1, P]], channel_multiplier=-1).then_inc(s["consts_pool"], 1)
            E.affine_select(out=ident[:, :], in_=ident[:, :], compare_op=ALU.not_equal, fill=1.0, base=0,
                            pattern=[[-1, P]], channel_multiplier=1).then_inc(s["consts_pool"], 1)
            pool.wait_ge(s["cols_ready"], 1)
            for k in range(KT):
                E.tensor_scalar(lnb_wide[:, k, :], lnb_wide[:, k, :], lnb_cols[:, k:k + 1], 0.0,
                                ALU.mult, ALU.add).then_inc(s["wide"], 1)
            def tiny(out_, a, b, op, sem_):
                E.tensor_tensor(out_, a, b, op).then_inc(sem_, 1)

            def small_stats(c):
                if not c.exists:
                    return
                var, r, done = moments[:, c.slot, 1:2], small[:, c.slot, :], s["x_small"]
                pool.wait_ge(s["x_stats"], c.done(2, 2))
                wait(pool, s["value_ready"], Chunk(c.p, c.off - 4).done())
                tiny(r[:, 0:1], var, eps_col[:, :], ALU.add, done)
                pool.wait_ge(done, c.done(6, 1))
                tiny(r[:, 1:2], r[:, 0:1], minus_half[:, :], ALU.pow, done)
                pool.wait_ge(done, c.done(6, 2))
                tiny(r[:, 2:3], r[:, 1:2], r[:, 1:2], ALU.mult, done)
                pool.wait_ge(done, c.done(6, 3))
                tiny(r[:, 3:4], r[:, 2:3], var, ALU.mult, done)
                pool.wait_ge(done, c.done(6, 4))
                tiny(r[:, 5:6], r[:, 3:4], eps_col[:, :], ALU.add, done)
                pool.wait_ge(done, c.done(6, 5))
                tiny(r[:, 4:5], r[:, 5:6], minus_half[:, :], ALU.pow, done)

            def add_bias(c):
                if c.exists:
                    pool.wait_ge(s["z_ready"], c.done())
                    E.tensor_tensor(xs[:, c.slot, :], xs[:, c.slot, :], bias_proj[:, :], ALU.add)\
                        .then_inc(s["xb_ready"], 1)

            pool.wait_ge(s["consts_pool"], 7)
            small_stats(Chunk(0, 0))
            small_stats(Chunk(0, 1))
            pool.wait_ge(s["late_biases"], 16 * 2)
            add_bias(Chunk(0, 0))

            def h_tail(g, i):
                pool.wait_ge(s["h_hi_ready"], g.done(PAIRS, i + 1))
                E.tensor_tensor(h_lo[:, i % 2, :], h_full[:, i % 2, :], h_hi[:, i % 2, :].bitcast(F32),
                                ALU.subtract).then_inc(s["h_lo_ready"], 1)

            def step(p, b):
                n, c, d = Chunk(p, b), Chunk(p, b - 1), Chunk(p, b - 2)
                ffn = Group(p, (b - 3) // 2) if b % 2 else Group(p, (b - 4) // 2)
                pairs = range(4) if b % 2 else range(4, 8)
                if d.exists:
                    pool.wait_ge(s["z1_ready"], d.done())
                    E.tensor_tensor(x1s[:, d.slot, :], x1s[:, d.slot, :], bias_out[:, :], ALU.add)\
                        .then_inc(s["x1b_ready"], 1)
                if c.exists:
                    if c.first:
                        pool.wait_ge(s["query_zero"], 2)
                    if d.exists:
                        pool.wait_ge(s["x1b_ready"], d.done())
                    if Chunk(p, b + 1).exists:
                        pool.wait_ge(s["x_small"], Chunk(p, b + 1).done(6, 6))
                    elif n.exists:
                        pool.wait_ge(s["x1_small"], d.done(2, 2))
                    for j in range(HPG):
                        rows = slice(HEAD * j, HEAD * (j + 1))
                        pool.wait_ge(s["query_bd_hi_ready"], c.done(HPG, j + 1))
                        if j:
                            pool.wait_ge(s["query_bd_ready"], c.done(HPG, j))
                        E.tensor_tensor(query_bd_lo[rows, :, j, :], query_t[rows, :, :],
                                        query_bd_hi[rows, :, j, :].bitcast(F32), ALU.subtract)\
                            .then_inc(s["query_bd_ready"], 1)
                    pool.wait_ge(s["query_bd_ready"], c.done(HPG, HPG))
                if ffn.exists and b % 2 == 0 and not is_last(p):
                    h_tail(ffn, pairs[0])
                if n.exists:
                    eps_wide = eps_col[:, :].broadcast_to([P, DM])
                    pool.wait_ge(s["key_steps"], n.done(3, 3))
                    E.tensor_tensor(keys[:, n.half, :], keys[:, n.half, :], eps_wide, ALU.add)\
                        .then_inc(s["key_ready"], 1)
                    pool.wait_ge(s["query_steps"], n.done(3, 3))
                    E.tensor_tensor(queries[:, :], queries[:, :], eps_wide, ALU.add)\
                        .then_inc(s["query_ready"], 1)
                if ffn.exists and not is_last(p):
                    if b % 2:
                        h_tail(ffn, pairs[0])
                    h_tail(ffn, pairs[1])
                add_bias(Chunk(p, b + 1))
                if n.exists:
                    pool.wait_ge(s["key_hi_ready"], n.done())
                    E.tensor_tensor(key_lo[:, :], keys[:, n.half, :], key_hi[:, :].bitcast(F32),
                                    ALU.subtract).then_inc(s["key_lo_ready"], 1)
                if ffn.exists and not is_last(p):
                    h_tail(ffn, pairs[2])
                    h_tail(ffn, pairs[3])
                if c.exists:
                    pool.wait_ge(s["x1_steps"], c.done(3, 3))
                    wait(pool, s["z1_ready"], d.done())
                    tiny(small1[:, 0:1], moments1[:, 1:2], eps_col[:, :], ALU.add, s["x1_small"])
                    pool.wait_ge(s["x1_small"], c.done(2, 1))
                    tiny(small1[:, 1:2], small1[:, 0:1], minus_half[:, :], ALU.pow, s["x1_small"])
                small_stats(Chunk(p, b + 2))

            steps(pool, step)

        @block.scalar
        def _(act):
            E = nc.scalar
            act.dma_start(bias[:, GATE, :], b_gate.rearrange("(a n) -> a n", a=1).broadcast_to([P, DM]))\
                .then_inc(s["biases"], 16)
            act.wait_ge(s["vectors_turned"], 1)
            E.activation(cols[:, :], ps_q[:, 0:FT + 2 * KT], ACT.Copy).then_inc(s["cols_ready"], 1)
            act.wait_ge(s["cols_ready"], 1)
            def z_head(c):
                if c.exists:
                    act.wait_ge(s["tz_done"], c.done())
                    E.activation(zt_hi[:, :, :].rearrange(flat), ps_t[:, :], ACT.Copy)\
                        .then_inc(s["zt_hi_ready"], 1)

            def tile_heads(ts):
                for t in ts:
                    _, hi, _, k, _ = tiles[t]
                    act.wait_ge(stage_in[t % 6], 16 * (t // 6 + 1))
                    scale = 1.0 if k is None else g_cols[:, k:k + 1]
                    E.activation(hi, stage(t), ACT.Copy, scale=scale).then_inc(s["stage_hi"], 1)

            tile_heads(range(KT))
            z_head(Chunk(0, 0))
            tile_heads(range(KT, 6))
            b_row = b_qkv.rearrange("(a n) -> a n", a=1)
            for group, third in ((KEY, 1), (QUERY, 0), (VALUE, 2)):
                act.dma_start(bias[:, group, :], b_row[:, third * DM:(third + 1) * DM].broadcast_to([P, DM]))\
                    .then_inc(s["biases"], 16)
            tile_heads(range(6, FIRST))
            act.dma_start(bias_proj[:, :], b_proj.rearrange("(a n) -> a n", a=1).broadcast_to([P, DM]))\
                .then_inc(s["late_biases"], 16)
            act.dma_start(bias_out[:, :], b2.rearrange("(a n) -> a n", a=1).broadcast_to([P, DM]))\
                .then_inc(s["late_biases"], 16)

            def gelu(g, i):
                act.wait_ge(s["h_done"], g.done(PAIRS, i + 1))
                for a in range(2):
                    last = E.activation(h_full[:, i % 2, a * GROUP:(a + 1) * GROUP],
                                        ps_h[i % 2][:, a * GROUP:(a + 1) * GROUP], ACT.Gelu_apprx_tanh,
                                        bias=b1_cols[:, 2 * i + a:2 * i + a + 1])
                last.then_inc(s["h_full_ready"], 1)

            def step(p, b):
                n, c, d = Chunk(p, b), Chunk(p, b - 1), Chunk(p, b - 2)
                ffn = Group(p, (b - 3) // 2) if b % 2 else Group(p, (b - 4) // 2)
                pairs = range(4) if b % 2 else range(4, 8)
                if c.exists:
                    act.wait_ge(s["tq_done"], c.done())
                    E.activation(query_t.rearrange(flat), ps_t[:, :], ACT.Copy)\
                        .then_inc(s["query_t_ready"], 1)
                if n.exists:
                    act.wait_ge(s["gate_evac"], n.done())
                    E.activation(gate[:, :], gate[:, :], ACT.Sigmoid, accum_out=gate_sum[:, :])\
                        .then_inc(s["gate_sig"], 1)
                if isinstance(p, int) and 4 * p + b == 0:
                    tile_heads(early_tiles)
                if d.exists:
                    act.wait_ge(s["tx_done"], d.done())
                    E.activation(x1t_hi[:, :, d.half * P:(d.half + 1) * P],
                                 ps_t[:, :].rearrange("p (k n) -> p k n", k=KT), ACT.Copy)\
                        .then_inc(s["x1t_hi_ready"], 1)
                if c.exists:
                    if c.first:
                        act.wait_ge(s["query_zero"], 2)
                    act.wait_ge(s["query_t_ready"], c.done())
                    for j in range(HPG):
                        rows = slice(HEAD * j, HEAD * (j + 1))
                        E.activation(query_bd_hi[rows, :, j, :], query_t[rows, :, :], ACT.Copy)\
                            .then_inc(s["query_bd_hi_ready"], 1)
                if c.exists:
                    act.wait_ge(s["tk_done"], c.done())
                    E.activation(key_t_hi[:, :, :].rearrange(flat), ps_t[:, :], ACT.Copy)\
                        .then_inc(s["key_t_hi_ready"], 1)
                if b % 2 and ffn.exists:
                    act.wait_ge(s["p_done"], ffn.done())
                    E.activation(pt_hi[:, :], ps_c[:, 0:GROUP], ACT.Copy).then_inc(s["pt_hi_ready"], 1)
                if ffn.exists and b % 2 == 0:
                    gelu(ffn, pairs[0])
                if ffn.exists and b % 2:
                    gelu(ffn, pairs[0])
                if ffn.exists:
                    gelu(ffn, pairs[1])
                if n.exists:
                    act.wait_ge(s["key_ready"], n.done())
                    if c.exists:
                        if not c.first:
                            act.wait_ge(s["earlier_done"], Chunk(c.p, c.off - 4).done())
                        act.wait_ge(s["query_bd_ready"], c.done(HPG, HPG))
                    E.activation(key_hi[:, :], keys[:, n.half, :], ACT.Copy).then_inc(s["key_hi_ready"], 1)
                if ffn.exists:
                    gelu(ffn, pairs[2])
                if c.exists:
                    act.wait_ge(s["ot_done"], c.done())
                    E.activation(ot_hi[:, :, :].rearrange(flat), ps_b[:, :], ACT.Copy)\
                        .then_inc(s["ot_hi_ready"], 1)
                z_head(Chunk(p, b + 1))
                if ffn.exists:
                    gelu(ffn, pairs[3])
                    if b % 2 == 0:
                        act.wait_ge(s["qacc_done"], ffn.done())
                        E.activation(qt_hi[:, :], ps_q[:, 0:GROUP], ACT.Copy).then_inc(s["qt_hi_ready"], 1)
                if isinstance(p, int) and 4 * p + b < 3:
                    tile_heads(late_tiles[b])

            steps(act, step)

        @block.vector
        def _(dve):
            E = nc.vector

            def x_stats_wait(c):
                if c.exists:
                    dve.wait_ge(x_in[c.slot], c.dmas())
                    wait(dve, s["x_small"], Chunk(c.p, c.off - 4).done(6, 6))

            def x_stats(c):
                if c.exists:
                    E.bn_stats(stats[:, c.slot, :], xs[:, c.slot, :]).then_inc(s["x_stats"], 1)

            def x_moments(c):
                if c.exists:
                    E.bn_aggr(moments[:, c.slot, :], stats[:, c.slot, :]).then_inc(s["x_stats"], 1)

            def x_norm(c):
                if c.exists:
                    dve.wait_ge(s["x_small"], c.done(6, 2))
                    before = Chunk(c.p, c.off - 3)
                    if before.exists:
                        dve.wait_ge(s["tx_done"], before.done())
                    E.tensor_scalar(zs[:, :], xs[:, c.slot, :], moments[:, c.slot, 0:1], small[:, c.slot, 1:2],
                                    ALU.subtract, ALU.mult).then_inc(s["z_ready"], 1)

            for half in (query_bd_hi, query_bd_lo):
                E.memset(half[:, :, :, :].rearrange("p k j n -> p (k j n)").bitcast(F32), 0.0)\
                    .then_inc(s["query_zero"], 1)
            E.memset(state_bd[:, :, :, :].rearrange("p b k n -> p (b k n)"), 0.0).then_inc(s["state_zero"], 1)
            def first_stats(m):
                x_stats_wait(Chunk(0, m))
                x_stats(Chunk(0, m))
                dve.wait_ge(s["x_stats"], 2 * m + 1)
                x_moments(Chunk(0, m))

            first_stats(0)
            x_norm(Chunk(0, 0))
            dve.wait_ge(s["cols_ready"], 1)
            def z_tail(c):
                if c.exists:
                    dve.wait_ge(s["zt_hi_ready"], c.done())
                    E.tensor_tensor(zt_lo[:, :, :].rearrange(flat), ps_t[:, :],
                                    zt_hi[:, :, :].rearrange(flat).bitcast(F32), ALU.subtract)\
                        .then_inc(s["zt_ready"], 1)

            def tile_tails(ts):
                for t in ts:
                    _, hi, lo, k, _ = tiles[t]
                    dve.wait_ge(s["stage_hi"], t + 1)
                    if k is None:
                        E.tensor_tensor(lo, stage(t), hi.bitcast(F32), ALU.subtract)\
                            .then_inc(s["stage_lo"], 1)
                    else:
                        E.scalar_tensor_tensor(out=lo, in0=stage(t), scalar=g_cols[:, k:k + 1],
                                               in1=hi.bitcast(F32), op0=ALU.mult, op1=ALU.subtract)\
                            .then_inc(s["stage_lo"], 1)

            tile_tails(range(KT))
            z_tail(Chunk(0, 0))
            tile_tails(range(KT, 10))
            first_stats(1)
            tile_tails(range(10, FIRST))
            dve.wait_ge(s["biases"], 16 * 4)
            for i, group in enumerate(bias_order):
                dve.wait_ge(s["stage_bias"], KT * (i + 1))
                ps = bias_banks[i]
                E.tensor_tensor(bias[:, group, :], ps[:, :], bias[:, group, :], ALU.add)\
                    .then_inc(s["bias_ready"], 1)
            dve.wait_ge(s["bias_ready"], 3)

            def squared_relu(n, done, chain, ps, group, dst, between=lambda: None):
                dve.wait_ge(done, n.done())
                E.scalar_tensor_tensor(out=dst, in0=ps[:, :], scalar=small[:, n.slot, 4:5],
                                       in1=bias[:, group, :], op0=ALU.mult, op1=ALU.add).then_inc(chain, 1)
                dve.wait_ge(chain, n.done(3, 1))
                E.scalar_tensor_tensor(out=dst, in0=dst, scalar=gate_scale[:, 1:2], in1=gate[:, :],
                                       op0=ALU.mult, op1=ALU.mult).then_inc(chain, 1)
                between()
                dve.wait_ge(chain, n.done(3, 2))
                E.scalar_tensor_tensor(out=dst, in0=dst, scalar=0.0, in1=dst, op0=ALU.max, op1=ALU.mult)\
                    .then_inc(chain, 1)

            def h_head(g, i, tail=False):
                dve.wait_ge(s["h_full_ready"], g.done(PAIRS, i + 1))
                E.tensor_copy(h_hi[:, i % 2, :], h_full[:, i % 2, :]).then_inc(s["h_hi_ready"], 1)
                if tail:
                    dve.wait_ge(s["h_hi_ready"], g.done(PAIRS, i + 1))
                    dve.wait_ge(s["h_lo_ready"], g.done(PAIRS, i))
                    E.tensor_tensor(h_lo[:, i % 2, :], h_full[:, i % 2, :], h_hi[:, i % 2, :].bitcast(F32),
                                    ALU.subtract).then_inc(s["h_lo_ready"], 1)

            def step(p, b):
                n, c, d = Chunk(p, b), Chunk(p, b - 1), Chunk(p, b - 2)
                ffn = Group(p, (b - 3) // 2) if b % 2 else Group(p, (b - 4) // 2)
                pairs = range(4) if b % 2 else range(4, 8)
                finishing = is_last(p)
                def x1t_tail():
                    if d.exists:
                        dve.wait_ge(s["x1t_hi_ready"], d.done())
                        part = slice(d.half * P, (d.half + 1) * P)
                        E.tensor_tensor(x1t_lo[:, :, part], ps_t[:, :].rearrange("p (k n) -> p k n", k=KT),
                                        x1t_hi[:, :, part].bitcast(F32), ALU.subtract).then_inc(s["x1t_ready"], 1)

                if n.exists:
                    dve.wait_ge(s["gate_done"], n.done())
                    E.tensor_tensor(gate[:, :], ps_b[:, :], bias[:, GATE, :], ALU.add)\
                        .then_inc(s["gate_evac"], 1)
                    dve.wait_ge(s["gate_sig"], n.done())
                    E.tensor_scalar(gate_scale[:, 0:1], gate_sum[:, :], 1.0 / DM, EPS, ALU.mult, ALU.add)\
                        .then_inc(s["gate_scale_ready"], 1)
                    dve.wait_ge(s["gate_scale_ready"], n.done(2, 1))
                    E.reciprocal(gate_scale[:, 1:2], gate_scale[:, 0:1]).then_inc(s["gate_scale_ready"], 1)
                    dve.wait_ge(s["gate_scale_ready"], n.done(2, 2))
                    dve.wait_ge(s["x_small"], n.done(6, 6))
                    squared_relu(n, s["key_done"], s["key_steps"], ps_a, KEY, keys[:, n.half, :],
                                 x1t_tail)
                else:
                    x1t_tail()
                if b % 2:
                    g = Group(p, (b - 5) // 2)
                    for a in range(2):
                        if g.exists:
                            r = g.chunk(a)
                            ps = (ps_c, ps_d)[a]
                            dve.wait_ge(s["result_done"], g.done(2, a + 1))
                            dve.wait_ge(s["x1b_ready"], r.done())
                            E.tensor_tensor(x1s[:, r.slot, :], ps[:, :], x1s[:, r.slot, :], ALU.add)\
                                .then_inc(s["result_ready"], 1)
                if n.exists:
                    if c.exists:
                        dve.wait_ge(s["tq_done"], c.done())
                    squared_relu(n, s["query_done"], s["query_steps"], ps_b, QUERY, queries[:, :])
                x_norm(Chunk(p, b + 1))
                if c.exists:
                    dve.wait_ge(s["key_t_hi_ready"], c.done())
                    E.tensor_tensor(key_t_lo[:, :, :].rearrange(flat), ps_t[:, :],
                                    key_t_hi[:, :, :].rearrange(flat).bitcast(F32), ALU.subtract)\
                        .then_inc(s["key_t_ready"], 1)
                if b % 2 and ffn.exists:
                    dve.wait_ge(s["pt_hi_ready"], ffn.done())
                    E.tensor_tensor(pt_lo[:, :], ps_c[:, 0:GROUP], pt_hi[:, :].bitcast(F32), ALU.subtract)\
                        .then_inc(s["pt_ready"], 1)
                if ffn.exists and b % 2 == 0:
                    h_head(ffn, pairs[0], finishing)
                if n.exists:
                    dve.wait_ge(s["value_done"], n.done())
                    E.scalar_tensor_tensor(out=values[:, n.half, :], in0=ps_a[:, :],
                                           scalar=small[:, n.slot, 4:5], in1=bias[:, VALUE, :],
                                           op0=ALU.mult, op1=ALU.add).then_inc(s["value_ready"], 1)
                if isinstance(p, int) and 4 * p + b == 0:
                    tile_tails(early_tiles)
                if ffn.exists and b % 2:
                    h_head(ffn, pairs[0], finishing)
                if ffn.exists:
                    h_head(ffn, pairs[1], finishing)
                if c.exists:
                    for ft in range(KT):
                        ps = (ps_c, ps_d)[ft % 2]
                        dve.wait_ge(s["scores_done"], c.done(KT, ft + 1))
                        E.tensor_tensor(probs[:, ft % 2, :].rearrange("p (j t) -> p j t", j=HPG),
                                        ps[:, :].rearrange("p (j t) -> p j t", j=HPG),
                                        causal.unsqueeze(1).broadcast_to([P, HPG, P]), ALU.mult)\
                            .then_inc(s["probs_ready"], 1)
                        if ft == 2 and ffn.exists:
                            h_head(ffn, pairs[2], finishing)
                    dve.wait_ge(s["state_done"], c.done())
                    for j in range(HPG):
                        q = slice(HEAD * j, HEAD * (j + 1))
                        mine = state_bd[q, c.slot, :, q]
                        new = ps_c[:, :].rearrange("p (k n) -> p k n", k=KT)[q, :, q]
                        last = E.tensor_tensor(mine, new, mine, ALU.add)
                    last.then_inc(s["state_ready"], 1)
                    dve.wait_ge(s["ot_hi_ready"], c.done())
                    E.tensor_tensor(ot_lo[:, :, :].rearrange(flat), ps_b[:, :],
                                    ot_hi[:, :, :].rearrange(flat).bitcast(F32), ALU.subtract)\
                        .then_inc(s["ot_ready"], 1)
                elif ffn.exists:
                    h_head(ffn, pairs[2], finishing)
                z_tail(Chunk(p, b + 1))
                if ffn.exists:
                    h_head(ffn, pairs[3], finishing)
                if n.exists:
                    den_steps = s["den_steps"]
                    dve.wait_ge(s["sums_done"], n.done())
                    if c.exists:
                        dve.wait_ge(carry_out[c.slot], c.dmas())
                    if n.first:
                        E.tensor_copy(key_sums[:, :], ps_b[:, :]).then_inc(den_steps, 1)
                    else:
                        dve.wait_ge(s["carry_in"], Chunk(n.p, n.off - 4).done(16, 16))
                        E.tensor_tensor(key_sums[:, :], ps_b[:, :], key_sums[:, :], ALU.add).then_inc(den_steps, 1)
                    dve.wait_ge(den_steps, n.done(6, 1))
                    dve.wait_ge(s["query_ready"], n.done())
                    E.tensor_tensor(gate[:, :], key_sums[:, :], queries[:, :], ALU.mult).then_inc(den_steps, 1)
                    dve.wait_ge(den_steps, n.done(6, 2))
                    E.tensor_reduce(den[:, 0, :], gate[:, :].rearrange("p (h d) -> p h d", d=HEAD), AX.X,
                                    ALU.add).then_inc(den_steps, 1)
                    dve.wait_ge(den_steps, n.done(6, 3))
                    E.tensor_scalar(den[:, 1, :], den[:, 0, :], EPS, None, ALU.add).then_inc(den_steps, 1)
                    dve.wait_ge(den_steps, n.done(6, 4))
                    E.reciprocal(den[:, 2, :], den[:, 1, :]).then_inc(den_steps, 1)
                    dve.wait_ge(den_steps, n.done(6, 5))
                    by_head = queries[:, :].rearrange("p (h d) -> p h d", d=HEAD)
                    E.tensor_tensor(by_head, by_head, den[:, 2, :].unsqueeze(2).broadcast_to([P, NH, HEAD]),
                                    ALU.mult).then_inc(den_steps, 1)
                if c.exists:
                    dve.wait_ge(s["y_done"], c.done())
                    dve.wait_ge(s["xb_ready"], c.done())
                    before = Chunk(c.p, c.off - 4)
                    if before.exists:
                        dve.wait_ge(stored[c.slot], before.dmas())
                    E.tensor_tensor(x1s[:, c.slot, :], ps_a[:, :], xs[:, c.slot, :], ALU.add)\
                        .then_inc(s["x1_steps"], 1)
                    dve.wait_ge(s["x1_steps"], c.done(3, 1))
                    E.bn_stats(stats1[:, :], x1s[:, c.slot, :]).then_inc(s["x1_steps"], 1)
                    dve.wait_ge(s["x1_steps"], c.done(3, 2))
                    wait(dve, s["x1_small"], d.done(2, 2))
                ahead = Chunk(p, b + 2)
                x_stats_wait(ahead)
                x_stats(ahead)
                if c.exists:
                    E.bn_aggr(moments1[:, :], stats1[:, :]).then_inc(s["x1_steps"], 1)
                if ahead.exists:
                    dve.wait_ge(s["x_stats"], ahead.done(2, 1))
                if c.exists:
                    dve.wait_ge(s["x1_small"], c.done(2, 2))
                    after = Chunk(p, b + 1)
                    if after.exists:
                        dve.wait_ge(s["tz_done"], after.done())
                    elif d.exists:
                        dve.wait_ge(s["tx_done"], d.done())
                    E.tensor_scalar(zs[:, :], x1s[:, c.slot, :], moments1[:, 0:1], small1[:, 1:2],
                                    ALU.subtract, ALU.mult).then_inc(s["z1_ready"], 1)
                x_moments(ahead)
                if ffn.exists and b % 2 == 0:
                    dve.wait_ge(s["qt_hi_ready"], ffn.done())
                    E.tensor_tensor(qt_lo[:, :], ps_q[:, 0:GROUP], qt_hi[:, :].bitcast(F32), ALU.subtract)\
                        .then_inc(s["qt_ready"], 1)
                if isinstance(p, int) and 4 * p + b < 3:
                    tile_tails(late_tiles[b])

            steps(dve, step)

        @block.tensor
        def _(pe):
            E = nc.tensor

            def product(ps, weights, moving, start=True, stop=True):
                last = len(weights) - 1
                for i, ((wh, wl), (mh, ml)) in enumerate(zip(weights, moving)):
                    E.matmul(ps, wh, mh, start=start and i == 0, stop=False)
                    E.matmul(ps, wh, ml, start=False, stop=False)
                    mm = E.matmul(ps, wl, mh, start=False, stop=stop and i == last)
                return mm

            def transpose4(src, done):
                for k in range(KT):
                    mm = E.transpose(ps_t[:, k * P:(k + 1) * P], src[:, k * P:(k + 1) * P], ident[:, :])
                mm.then_inc(done, 1)

            def project(group, ps, done):
                product(ps[:, :], [(zt_hi[:, k, :], zt_lo[:, k, :]) for k in range(KT)],
                        [(wx_hi[:, k, group, :], wx_lo[:, k, group, :]) for k in range(KT)]).then_inc(done, 1)

            pe.wait_ge(s["vectors"], 48)
            pe.wait_ge(s["consts_pool"], 7)
            rows = FT + 2 * KT
            E.transpose(ps_q[:, 0:rows], vector_rows, ident[0:rows, 0:rows]).then_inc(s["vectors_turned"], 1)
            def bias_products(i):
                if i == 0:
                    pe.wait_ge(s["wide"], KT)
                for t in with_bias[KT * i:KT * (i + 1)]:
                    k = tiles[t][3]
                    pe.wait_ge(stage_in[t % 6], 16 * (t // 6 + 1))
                    E.matmul(bias_banks[i][:, :], lnb_wide[:, k, :], stage(t), start=k == 0, stop=k == KT - 1)\
                        .then_inc(s["stage_bias"], 1)

            def tz(c):
                if not c.exists:
                    return
                pe.wait_ge(s["z_ready"], c.done())
                before = Chunk(c.p, c.off - 2)
                if before.exists:
                    pe.wait_ge(s["key_t_ready"], before.done())
                transpose4(zs, s["tz_done"])

            tz(Chunk(0, 0))
            bias_products(0)

            def h_pair(g, i):
                if i == 0:
                    pe.wait_ge(s["pt_ready"], g.done())
                if i >= 2:
                    pe.wait_ge(s["h_full_ready"], g.done(PAIRS, i - 1))
                else:
                    wait(pe, s["h_full_ready"], Group(g.p, g.off - 1).done(PAIRS, PAIRS - 1 + i))
                for a in range(2):
                    j = 2 * i + a
                    mm = product(ps_h[i % 2][:, a * GROUP:(a + 1) * GROUP], [(v1_hi[:, j, :], v1_lo[:, j, :])],
                                 [(pt_hi[:, :], pt_lo[:, :])])
                mm.then_inc(s["h_done"], 1)

            def q_pair(g, i):
                pe.wait_ge(s["h_lo_ready"], g.done(PAIRS, i + 1))
                if i == 0:
                    wait(pe, s["qt_ready"], Group(g.p, g.off - 1).done())
                cols = [slice(a * GROUP, (a + 1) * GROUP) for a in range(2)]
                mm = product(ps_q[:, 0:GROUP], [(u2_hi[:, 2 * i + a, :], u2_lo[:, 2 * i + a, :]) for a in range(2)],
                             [(h_hi[:, i % 2, q], h_lo[:, i % 2, q]) for q in cols],
                             start=i == 0, stop=i == PAIRS - 1)
                if i == PAIRS - 1:
                    mm.then_inc(s["qacc_done"], 1)

            def step(p, b):
                n, c, d = Chunk(p, b), Chunk(p, b - 1), Chunk(p, b - 2)
                ffn = Group(p, (b - 3) // 2) if b % 2 else Group(p, (b - 4) // 2)
                result = Group(p, (b - 5) // 2) if b % 2 else None
                pairs = range(4) if b % 2 else range(4, 8)
                if n.exists:
                    pe.wait_ge(s["zt_ready"], n.done())
                    if c.exists:
                        pe.wait_ge(s["den_steps"], c.done(6, 1))
                    else:
                        bias_products(1)
                        pe.wait_ge(s["stage_lo"], KT)
                    project(GATE, ps_b, s["gate_done"])
                    if not c.exists:
                        bias_products(2)
                        pe.wait_ge(s["stage_lo"], 2 * KT)
                if c.exists:
                    pe.wait_ge(s["den_steps"], c.done(6, 6))
                    if n.exists:
                        pe.wait_ge(s["zt_ready"], n.done())
                    else:
                        pe.wait_ge(s["key_t_ready"], d.done())
                    transpose4(queries, s["tq_done"])
                if n.exists:
                    if d.exists:
                        pe.wait_ge(s["x1_steps"], d.done(3, 1))
                    project(KEY, ps_a, s["key_done"])
                    if not c.exists:
                        pe.wait_ge(s["stage_lo"], FIRST)
                if d.exists:
                    pe.wait_ge(s["z1_ready"], d.done())
                    if c.exists:
                        pe.wait_ge(s["query_t_ready"], c.done())
                    else:
                        pe.wait_ge(s["key_t_ready"], d.done())
                    transpose4(zs, s["tx_done"])
                if result is not None and result.exists:
                    pe.wait_ge(s["qt_ready"], result.done())
                    for a in range(2):
                        cols = slice(a * P, (a + 1) * P)
                        ps = (ps_c, ps_d)[a]
                        before = d if d.exists else Chunk(0, CHUNKS - 1)
                        if a:
                            pe.wait_ge(s["probs_ready"], before.done(KT, KT))
                        else:
                            pe.wait_ge(s["state_ready"], before.done())
                        product(ps[:, :], [(qt_hi[:, cols], qt_lo[:, cols])], [(v2_hi[:, :], v2_lo[:, :])])\
                            .then_inc(s["result_done"], 1)
                if n.exists:
                    pe.wait_ge(s["gate_evac"], n.done())
                    project(QUERY, ps_b, s["query_done"])
                if c.exists:
                    if d.exists:
                        pe.wait_ge(s["x1t_ready"], d.done())
                    else:
                        pe.wait_ge(s["query_t_ready"], c.done())
                    pe.wait_ge(s["key_ready"], c.done())
                    transpose4(keys[:, c.half, :], s["tk_done"])
                if b % 2 and ffn.exists:
                    if isinstance(p, int) and p == 0:
                        pe.wait_ge(s["stage_lo"], len(tiles))
                    pe.wait_ge(s["x1t_ready"], d.done())
                    pe.wait_ge(s["state_ready"], d.done())
                    if result.exists:
                        pe.wait_ge(s["result_ready"], result.chunk(0).done())
                    product(ps_c[:, 0:GROUP], [(u1_hi[:, k, :], u1_lo[:, k, :]) for k in range(KT)],
                            [(x1t_hi[:, k, :], x1t_lo[:, k, :]) for k in range(KT)]).then_inc(s["p_done"], 1)
                if ffn.exists and b % 2 == 0:
                    h_pair(ffn, pairs[0])
                if n.exists:
                    pe.wait_ge(s["key_steps"], n.done(3, 1))
                    project(VALUE, ps_a, s["value_done"])
                if ffn.exists and b % 2:
                    h_pair(ffn, pairs[0])
                if ffn.exists:
                    h_pair(ffn, pairs[1])
                if c.exists:
                    if n.exists:
                        pe.wait_ge(s["query_steps"], n.done(3, 1))
                    else:
                        pe.wait_ge(s["den_steps"], c.done(6, 1))
                    if not c.first:
                        pe.wait_ge(s["state_ready"], Chunk(c.p, c.off - 4).done())

                    def earlier(fts):
                        if not c.first:
                            for ft in fts:
                                mm = E.matmul(ps_b[:, ft * P:(ft + 1) * P], state_bd[:, c.slot, ft, :],
                                              query_t[:, ft, :], start=ft == 0, stop=False,
                                              skip_group_check=True)
                                if ft == KT - 1:
                                    mm.then_inc(s["earlier_done"], 1)

                    def scores(ft):
                        ps = (ps_c, ps_d)[ft % 2]
                        if ft >= 2:
                            pe.wait_ge(s["probs_ready"], c.done(KT, ft - 1))
                        else:
                            if result is not None and result.exists:
                                pe.wait_ge(s["result_ready"], result.chunk(ft).done())
                            if b % 2 and ffn.exists and ft == 0:
                                pe.wait_ge(s["pt_ready"], ffn.done())
                            if d.exists:
                                if ft == 0:
                                    pe.wait_ge(s["state_ready"], d.done())
                                else:
                                    pe.wait_ge(s["probs_ready"], d.done(KT, KT))
                        product(ps[:, :], [(key_t_hi[:, ft, :], key_t_lo[:, ft, :])],
                                [(query_bd_hi[:, ft, :, :].rearrange("p j t -> p (j t)"),
                                  query_bd_lo[:, ft, :, :].rearrange("p j t -> p (j t)"))])\
                            .then_inc(s["scores_done"], 1)

                    def mix(ft):
                        pe.wait_ge(s["probs_ready"], c.done(KT, ft + 1))
                        for j in range(HPG):
                            h = ft * HPG + j
                            mm = E.matmul(ps_b[HEAD * j:HEAD * (j + 1), ft * P:(ft + 1) * P],
                                          values[:, c.half, h * HEAD:(h + 1) * HEAD],
                                          probs[:, ft % 2, j * P:(j + 1) * P],
                                          start=c.first and ft == 0, stop=True,
                                          tile_position=(0, HEAD * j), skip_group_check=True)
                        return mm

                    earlier((0, 1))
                    pe.wait_ge(s["query_bd_ready"], c.done(HPG, HPG))
                    pe.wait_ge(s["key_t_ready"], c.done())
                    scores(0)
                    scores(1)
                    earlier((2, 3))
                    pe.wait_ge(s["value_ready"], c.done())
                if ffn.exists:
                    q_pair(ffn, pairs[0])
                if c.exists:
                    mix(0)
                    mix(1)
                if ffn.exists:
                    h_pair(ffn, pairs[2])
                if c.exists:
                    scores(2)
                    scores(3)
                if ffn.exists:
                    q_pair(ffn, pairs[1])
                if c.exists:
                    pe.wait_ge(s["probs_ready"], c.done(KT, 3))
                    for ft in range(KT):
                        cols = slice(ft * P, (ft + 1) * P)
                        mm = E.matmul(ps_c[:, cols], keys[:, c.half, cols], values[:, c.half, cols],
                                      start=True, stop=True)
                    mm.then_inc(s["state_done"], 1)
                    mix(2)
                    mix(3).then_inc(s["ot_done"], 1)
                tz(Chunk(p, b + 1))
                if ffn.exists:
                    h_pair(ffn, pairs[3])
                    q_pair(ffn, pairs[2])
                if n.exists:
                    if c.exists:
                        pe.wait_ge(s["ot_ready"], c.done())
                    pe.wait_ge(s["key_lo_ready"], n.done())
                    E.matmul(ps_b[:, :], causal_r[:, :], key_hi[:, :], start=True, stop=False)
                    E.matmul(ps_b[:, :], causal_r[:, :], key_lo[:, :], start=False, stop=True)\
                        .then_inc(s["sums_done"], 1)
                if c.exists:
                    if c.first:
                        pe.wait_ge(s["stage_lo"], FIRST + KT)
                    pe.wait_ge(s["ot_ready"], c.done())
                    if n.exists:
                        pe.wait_ge(s["value_ready"], n.done())
                    elif d.exists:
                        pe.wait_ge(s["x1_steps"], d.done(3, 1))
                    product(ps_a[:, :], [(ot_hi[:, k, :], ot_lo[:, k, :]) for k in range(KT)],
                            [(wp_hi[:, k, :], wp_lo[:, k, :]) for k in range(KT)]).then_inc(s["y_done"], 1)
                if ffn.exists:
                    q_pair(ffn, pairs[3])

            steps(pe, step)


_INS = ['L0_attn_x', 'L0_attn_ln_g', 'L0_attn_ln_b', 'L0_attn_W_qkv', 'L0_attn_b_qkv', 'L0_attn_W_gate',
        'L0_attn_b_gate', 'L0_attn_W_proj', 'L0_attn_b_proj', 'L0_ffn_U1', 'L0_ffn_V1', 'L0_ffn_b1',
        'L0_ffn_U2', 'L0_ffn_V2', 'L0_ffn_b2']


def kernel(**inputs):
    import numpy as _np
    import concourse.bacc as _bacc
    from concourse import mybir as _mybir
    from concourse.bass_utils import run_bass_kernel_spmd as _run

    nc = _bacc.Bacc("TRN2", target_bir_lowering=False, num_devices=1, dynamic_dma_scratch_size=64)
    arrays, args = {}, []
    for name in _INS:
        a = _np.ascontiguousarray(inputs[name])
        arrays[name] = a
        args.append(nc.dram_tensor(name, a.shape, _mybir.dt.from_np(a.dtype), kind="ExternalInput").ap())
    out = nc.dram_tensor("out", (BATCHES, SEQ, DM), _mybir.dt.float32, kind="ExternalOutput").ap()
    carry_dram = nc.dram_tensor("carry_rows", (BATCHES, DM), _mybir.dt.float32, kind="Internal").ap()
    block_kernel(nc, *args, out, carry_dram)
    r = _run(nc, [arrays], core_ids=[0])
    return r.results[0]["out"]
```
